# Optimizing a Trainium2 kernel written in Bass

```python
import numpy as np
import jax
import jax.numpy as jnp

def _softmax(x, axis=-1):
    return jax.nn.softmax(x, axis=axis)

def _gelu(x):
    return jax.nn.gelu(x, approximate=True)

def _silu(x):
    return jax.nn.silu(x)

def _sigmoid(x):
    return jax.nn.sigmoid(x)

def _layernorm(x, axis=-1, eps=1e-05):
    m = jnp.mean(x, axis=axis, keepdims=True)
    v = jnp.var(x, axis=axis, keepdims=True)
    return (x - m) / jnp.sqrt(v + eps)

def _scatter_add(tgt, idx, src, axis=0):
    return tgt.at[idx].add(src)

def _segment_sum(src, seg, n):
    return jax.ops.segment_sum(src, seg, n)
kernel_name = 'mk_decoder_preln_d1_seqx_r2_f2e85b'

def setup_inputs(seed: int=0):
    np.random.seed(seed)
    _w = jnp.asarray

    def _rec_inputs():
        import jax
        import jax.numpy as jnp
        _rk = jax.random.key(seed)
        x = -0.0002928 + 1 * jax.random.normal(jax.random.fold_in(_rk, 1), (2, 2048, 512), jnp.float32)
        _lenS = 2048 - jax.random.randint(jax.random.fold_in(_rk, 7), (2,), 0, max(1, 2048 // 4) + 1, jnp.int32)
        _lenS2 = 154 - jax.random.randint(jax.random.fold_in(_rk, 8), (2,), 0, max(1, 154 // 4) + 1, jnp.int32)
        _ctx_1024P = jax.random.normal(jax.random.fold_in(_rk, 11), (2, 16, 512), jnp.float32)
        _ctx_1024c = jax.random.dirichlet(jax.random.fold_in(_rk, 511), 0.3 * jnp.ones((16,), jnp.float32), (2, 154))
        _ctx_1024t = jnp.einsum('bsk,bkd->bsd', _ctx_1024c, _ctx_1024P)
        _ctx_1024t = _ctx_1024t * jax.lax.rsqrt(jnp.mean(jnp.square(_ctx_1024t)) + 1e-12) * 0.953939
        ctx_1024 = -1.39393e-06 + 0.999914 * (_ctx_1024t + 0.3 * jax.random.normal(jax.random.fold_in(_rk, 611), (2, 154, 512), jnp.float32))
        _validS = jnp.arange(2048)[None, :] < _lenS[:, None]
        _validS2 = jnp.arange(154)[None, :] < _lenS2[:, None]
        _causal = jnp.tril(jnp.ones((2048, 2048), dtype=bool))
        mask_BxS2_bf0 = jnp.logical_not(jnp.ones((2, 154), dtype=bool))
        return (x, ctx_1024, mask_BxS2_bf0)
    x, ctx_1024, mask_BxS2_bf0 = _rec_inputs()

    def _L0_attn_setup():
        import jax, jax.numpy as jnp
        import numpy as np
        import math
        B, S, D = (2, 2048, 512)
        H = 16
        HEAD_DIM = D // H
        BLOCK = 512

        def _attention(x, w_qkv):
            b, s, d = x.shape
            hd = d // H
            nblk = s // BLOCK
            qkv = (x @ w_qkv.T).reshape(b, s, 3, H, hd)
            qkv = jnp.moveaxis(qkv, (2, 3), (0, 2))
            q, k, v = (qkv[0], qkv[1], qkv[2])
            kb = jnp.moveaxis(k.reshape(b, H, nblk, BLOCK, hd), 2, 0)
            vb = jnp.moveaxis(v.reshape(b, H, nblk, BLOCK, hd), 2, 0)
            scale = 1.0 / math.sqrt(hd)

            def step(carry, kv):
                out, lse = carry
                k_blk, v_blk = kv
                scores = jnp.einsum('bhid,bhjd->bhij', q, k_blk) * scale
                block_max = scores.max(axis=-1)
                exp_s = jnp.exp(scores - block_max[..., None])
                block_lse = block_max + jnp.log(exp_s.sum(axis=-1))
                new_lse = jnp.logaddexp(lse, block_lse)
                out = jnp.exp(lse - new_lse)[..., None] * out + jnp.exp(block_max - new_lse)[..., None] * jnp.einsum('bhij,bhjd->bhid', exp_s, v_blk)
                return ((out, new_lse), None)
            out0 = jnp.zeros_like(q)
            lse0 = jnp.full((b, H, s), -1e+30, dtype=x.dtype)
            (out, _), _ = jax.lax.scan(step, (out0, lse0), (kb, vb))
            return jnp.moveaxis(out, 1, 2).reshape(b, s, d)
        key = jax.random.key(seed)
        k1, k2, k3 = jax.random.split(key, 3)
        x = jax.random.normal(k1, (B, S, D), dtype=jnp.float32)
        w_qkv = jax.random.normal(k2, (3 * D, D), dtype=jnp.float32) * 0.02
        w_out = jax.random.normal(k3, (D, D), dtype=jnp.float32) * 0.02
        return {'x': x, 'w_qkv': w_qkv, 'w_out': w_out}
    _L0_attn_all = _L0_attn_setup()
    _L0_attn_in = {k: v for k, v in _L0_attn_all.items() if k in ('w_qkv', 'w_out')}
    del _L0_attn_all

    def _L0_xattn_setup():
        import jax, jax.numpy as jnp
        import numpy as np
        EMBED_DIM = 512
        NUM_HEADS = 16
        HEAD_DIM = EMBED_DIM // NUM_HEADS
        B, T, S = (2, 1024, 1024)
        key = jax.random.key(seed)
        ks = jax.random.split(key, 12)
        xavier = lambda k: jax.random.uniform(k, (EMBED_DIM, EMBED_DIM), jnp.float32, -np.sqrt(6.0 / (2 * EMBED_DIM)), np.sqrt(6.0 / (2 * EMBED_DIM)))
        return {'query': jax.random.normal(ks[0], (B, T, EMBED_DIM), jnp.float32), 'key': jax.random.normal(ks[1], (B, S, EMBED_DIM), jnp.float32), 'value': jax.random.normal(ks[2], (B, S, EMBED_DIM), jnp.float32), 'key_padding_mask': jnp.zeros((B, S), dtype=bool), 'Wq': xavier(ks[3]), 'bq': jnp.zeros((EMBED_DIM,), jnp.float32), 'Wk': xavier(ks[4]), 'bk': jnp.zeros((EMBED_DIM,), jnp.float32), 'Wv': xavier(ks[5]), 'bv': jnp.zeros((EMBED_DIM,), jnp.float32), 'Wo': xavier(ks[6]), 'bo': jnp.zeros((EMBED_DIM,), jnp.float32)}
    _L0_xattn_all = _L0_xattn_setup()
    _L0_xattn_in = {k: v for k, v in _L0_xattn_all.items() if k in ('Wq', 'bq', 'Wk', 'bk', 'Wv', 'bv', 'Wo', 'bo')}
    del _L0_xattn_all

    def _L0_ffn_setup():
        import jax, jax.numpy as jnp
        import numpy as np
        EPS = 1e-05

        def _ln(x, g, b):
            mu = jnp.mean(x, axis=-1, keepdims=True)
            var = jnp.mean(jnp.square(x - mu), axis=-1, keepdims=True)
            return (x - mu) * jax.lax.rsqrt(var + EPS) * g + b

        def _forward(x, index_b, index_t, sw1, sb1, sw2, sb2, sw3, sb3, s_ln_g, s_ln_b, sg_w, sg_b, eg_w, eg_b, exp_bias, ew1, eb1, ew2, eb2, ew3, eb3, sel_ln_g, sel_ln_b):
            x1 = jnp.einsum('btd,hd->bth', x, sw1) + sb1
            x2 = jnp.einsum('btd,hd->bth', x, sw2) + sb2
            sh = _ln(jax.nn.silu(x1) * x2, s_ln_g, s_ln_b)
            shared_out = jnp.einsum('bth,dh->btd', sh, sw3) + sb3
            x_moe = x[index_b, index_t]
            shared_scores = jax.nn.sigmoid(x_moe @ sg_w.T + sg_b)
            expert_scores = jax.nn.sigmoid(x_moe @ eg_w.T + eg_b)
            top1_idx = jnp.argmax(expert_scores + exp_bias, axis=-1)
            top1_score = jnp.take_along_axis(expert_scores, top1_idx[:, None], axis=-1)
            weights = jax.nn.softmax(jnp.concatenate([shared_scores, top1_score], axis=-1), axis=-1)
            shared_w, expert_w = (weights[:, 0], weights[:, 1])
            shared_moe_out = shared_out[index_b, index_t] * shared_w[:, None]
            h1 = jnp.einsum('md,ehd->meh', x_moe, ew1) + eb1
            h2 = jnp.einsum('md,ehd->meh', x_moe, ew2) + eb2
            z = _ln(jax.nn.silu(h1) * h2, sel_ln_g, sel_ln_b)
            out_all = jnp.einsum('meh,edh->med', z, ew3) + eb3
            expert_out = jnp.take_along_axis(out_all, top1_idx[:, None, None], axis=1)[:, 0]
            expert_moe_out = expert_out * expert_w[:, None]
            final_out = shared_out.at[index_b, index_t].set(shared_moe_out + expert_moe_out)
            return final_out
        B, T, D, E, H, M = (2, 1024, 512, 8, 256, 1024)
        key = jax.random.key(seed)
        ks = jax.random.split(key, 24)
        s = 0.02
        inp = {}
        inp['x'] = jax.random.normal(ks[0], (B, T, D), jnp.float32)
        flat = jnp.arange(M, dtype=jnp.int32) * 2
        inp['index_b'] = flat // T
        inp['index_t'] = flat % T
        inp['sw1'] = jax.random.normal(ks[1], (H, D), jnp.float32) * s
        inp['sb1'] = jnp.zeros((H,), jnp.float32)
        inp['sw2'] = jax.random.normal(ks[2], (H, D), jnp.float32) * s
        inp['sb2'] = jnp.zeros((H,), jnp.float32)
        inp['sw3'] = jax.random.normal(ks[3], (D, H), jnp.float32) * s
        inp['sb3'] = jnp.zeros((D,), jnp.float32)
        inp['s_ln_g'] = jnp.ones((H,), jnp.float32)
        inp['s_ln_b'] = jnp.zeros((H,), jnp.float32)
        inp['sg_w'] = jax.random.normal(ks[4], (1, D), jnp.float32) * s
        inp['sg_b'] = jnp.zeros((1,), jnp.float32)
        inp['eg_w'] = jax.random.normal(ks[5], (E, D), jnp.float32) * s
        inp['eg_b'] = jnp.zeros((E,), jnp.float32)
        inp['exp_bias'] = jnp.zeros((E,), jnp.float32)
        inp['ew1'] = jax.random.normal(ks[6], (E, H, D), jnp.float32) * s
        inp['eb1'] = jnp.zeros((E, H), jnp.float32)
        inp['ew2'] = jax.random.normal(ks[7], (E, H, D), jnp.float32) * s
        inp['eb2'] = jnp.zeros((E, H), jnp.float32)
        inp['ew3'] = jax.random.normal(ks[8], (E, D, H), jnp.float32) * s
        inp['eb3'] = jnp.zeros((E, D), jnp.float32)
        inp['sel_ln_g'] = jnp.ones((H,), jnp.float32)
        inp['sel_ln_b'] = jnp.zeros((H,), jnp.float32)
        return inp
    _L0_ffn_all = _L0_ffn_setup()
    _L0_ffn_in = {k: v for k, v in _L0_ffn_all.items() if k in ('index_b', 'index_t', 'sw1', 'sb1', 'sw2', 'sb2', 'sw3', 'sb3', 's_ln_g', 's_ln_b', 'sg_w', 'sg_b', 'eg_w', 'eg_b', 'exp_bias', 'ew1', 'eb1', 'ew2', 'eb2', 'ew3', 'eb3', 'sel_ln_g', 'sel_ln_b')}
    del _L0_ffn_all
    return {'x': x, 'ctx_1024': ctx_1024, 'mask_BxS2_bf0': mask_BxS2_bf0, 'L0_attn_w_qkv': _L0_attn_in['w_qkv'], 'L0_attn_w_out': _L0_attn_in['w_out'], 'L0_xattn_Wq': _L0_xattn_in['Wq'], 'L0_xattn_bq': _L0_xattn_in['bq'], 'L0_xattn_Wk': _L0_xattn_in['Wk'], 'L0_xattn_bk': _L0_xattn_in['bk'], 'L0_xattn_Wv': _L0_xattn_in['Wv'], 'L0_xattn_bv': _L0_xattn_in['bv'], 'L0_xattn_Wo': _L0_xattn_in['Wo'], 'L0_xattn_bo': _L0_xattn_in['bo'], 'L0_ffn_index_b': _L0_ffn_in['index_b'], 'L0_ffn_index_t': _L0_ffn_in['index_t'], 'L0_ffn_sw1': _L0_ffn_in['sw1'], 'L0_ffn_sb1': _L0_ffn_in['sb1'], 'L0_ffn_sw2': _L0_ffn_in['sw2'], 'L0_ffn_sb2': _L0_ffn_in['sb2'], 'L0_ffn_sw3': _L0_ffn_in['sw3'], 'L0_ffn_sb3': _L0_ffn_in['sb3'], 'L0_ffn_s_ln_g': _L0_ffn_in['s_ln_g'], 'L0_ffn_s_ln_b': _L0_ffn_in['s_ln_b'], 'L0_ffn_sg_w': _L0_ffn_in['sg_w'], 'L0_ffn_sg_b': _L0_ffn_in['sg_b'], 'L0_ffn_eg_w': _L0_ffn_in['eg_w'], 'L0_ffn_eg_b': _L0_ffn_in['eg_b'], 'L0_ffn_exp_bias': _L0_ffn_in['exp_bias'], 'L0_ffn_ew1': _L0_ffn_in['ew1'], 'L0_ffn_eb1': _L0_ffn_in['eb1'], 'L0_ffn_ew2': _L0_ffn_in['ew2'], 'L0_ffn_eb2': _L0_ffn_in['eb2'], 'L0_ffn_ew3': _L0_ffn_in['ew3'], 'L0_ffn_eb3': _L0_ffn_in['eb3'], 'L0_ffn_sel_ln_g': _L0_ffn_in['sel_ln_g'], 'L0_ffn_sel_ln_b': _L0_ffn_in['sel_ln_b']}

def reference(x, ctx_1024, mask_BxS2_bf0, L0_attn_w_qkv, L0_attn_w_out, L0_xattn_Wq, L0_xattn_bq, L0_xattn_Wk, L0_xattn_bk, L0_xattn_Wv, L0_xattn_bv, L0_xattn_Wo, L0_xattn_bo, L0_ffn_index_b, L0_ffn_index_t, L0_ffn_sw1, L0_ffn_sb1, L0_ffn_sw2, L0_ffn_sb2, L0_ffn_sw3, L0_ffn_sb3, L0_ffn_s_ln_g, L0_ffn_s_ln_b, L0_ffn_sg_w, L0_ffn_sg_b, L0_ffn_eg_w, L0_ffn_eg_b, L0_ffn_exp_bias, L0_ffn_ew1, L0_ffn_eb1, L0_ffn_ew2, L0_ffn_eb2, L0_ffn_ew3, L0_ffn_eb3, L0_ffn_sel_ln_g, L0_ffn_sel_ln_b):
    import jax
    import jax.numpy as jnp

    def _L0_attn_ref(x, w_qkv, w_out):
        import jax, jax.numpy as jnp
        import numpy as np
        import math
        B, S, D = (2, 2048, 512)
        H = 16
        HEAD_DIM = D // H
        BLOCK = 512

        def _attention(x, w_qkv):
            b, s, d = x.shape
            hd = d // H
            nblk = s // BLOCK
            qkv = (x @ w_qkv.T).reshape(b, s, 3, H, hd)
            qkv = jnp.moveaxis(qkv, (2, 3), (0, 2))
            q, k, v = (qkv[0], qkv[1], qkv[2])
            kb = jnp.moveaxis(k.reshape(b, H, nblk, BLOCK, hd), 2, 0)
            vb = jnp.moveaxis(v.reshape(b, H, nblk, BLOCK, hd), 2, 0)
            scale = 1.0 / math.sqrt(hd)

            def step(carry, kv):
                out, lse = carry
                k_blk, v_blk = kv
                scores = jnp.einsum('bhid,bhjd->bhij', q, k_blk) * scale
                block_max = scores.max(axis=-1)
                exp_s = jnp.exp(scores - block_max[..., None])
                block_lse = block_max + jnp.log(exp_s.sum(axis=-1))
                new_lse = jnp.logaddexp(lse, block_lse)
                out = jnp.exp(lse - new_lse)[..., None] * out + jnp.exp(block_max - new_lse)[..., None] * jnp.einsum('bhij,bhjd->bhid', exp_s, v_blk)
                return ((out, new_lse), None)
            out0 = jnp.zeros_like(q)
            lse0 = jnp.full((b, H, s), -1e+30, dtype=x.dtype)
            (out, _), _ = jax.lax.scan(step, (out0, lse0), (kb, vb))
            return jnp.moveaxis(out, 1, 2).reshape(b, s, d)
        attn = _attention(x, w_qkv)
        return attn @ w_out.T

    def _L0_xattn_ref(query, key, value, key_padding_mask, Wq, bq, Wk, bk, Wv, bv, Wo, bo):
        import jax, jax.numpy as jnp
        import numpy as np
        EMBED_DIM = 512
        NUM_HEADS = 16
        HEAD_DIM = EMBED_DIM // NUM_HEADS
        B, T, S = (2, 1024, 1024)
        bsz, tgt_len, _ = query.shape
        src_len = key.shape[1]
        q = (query @ Wq.T + bq).reshape(bsz, tgt_len, NUM_HEADS, HEAD_DIM).transpose(0, 2, 1, 3)
        k = (key @ Wk.T + bk).reshape(bsz, src_len, NUM_HEADS, HEAD_DIM).transpose(0, 2, 1, 3)
        v = (value @ Wv.T + bv).reshape(bsz, src_len, NUM_HEADS, HEAD_DIM).transpose(0, 2, 1, 3)
        scale = HEAD_DIM ** (-0.5)
        scores = jnp.einsum('bhtd,bhsd->bhts', q, k) * scale
        causal_mask = jnp.triu(jnp.ones((tgt_len, src_len), dtype=bool), k=1)
        neg_inf = jnp.finfo(scores.dtype).min
        scores = jnp.where(causal_mask[None, None], neg_inf, scores)
        scores = jnp.where(key_padding_mask[:, None, None, :], neg_inf, scores)
        attn = jax.nn.softmax(scores, axis=-1)
        out = jnp.einsum('bhts,bhsd->bhtd', attn, v)
        out = out.transpose(0, 2, 1, 3).reshape(bsz, tgt_len, EMBED_DIM)
        return out @ Wo.T + bo

    def _L0_ffn_ref(x, index_b, index_t, sw1, sb1, sw2, sb2, sw3, sb3, s_ln_g, s_ln_b, sg_w, sg_b, eg_w, eg_b, exp_bias, ew1, eb1, ew2, eb2, ew3, eb3, sel_ln_g, sel_ln_b):
        import jax, jax.numpy as jnp
        import numpy as np
        EPS = 1e-05

        def _ln(x, g, b):
            mu = jnp.mean(x, axis=-1, keepdims=True)
            var = jnp.mean(jnp.square(x - mu), axis=-1, keepdims=True)
            return (x - mu) * jax.lax.rsqrt(var + EPS) * g + b

        def _forward(x, index_b, index_t, sw1, sb1, sw2, sb2, sw3, sb3, s_ln_g, s_ln_b, sg_w, sg_b, eg_w, eg_b, exp_bias, ew1, eb1, ew2, eb2, ew3, eb3, sel_ln_g, sel_ln_b):
            x1 = jnp.einsum('btd,hd->bth', x, sw1) + sb1
            x2 = jnp.einsum('btd,hd->bth', x, sw2) + sb2
            sh = _ln(jax.nn.silu(x1) * x2, s_ln_g, s_ln_b)
            shared_out = jnp.einsum('bth,dh->btd', sh, sw3) + sb3
            x_moe = x[index_b, index_t]
            shared_scores = jax.nn.sigmoid(x_moe @ sg_w.T + sg_b)
            expert_scores = jax.nn.sigmoid(x_moe @ eg_w.T + eg_b)
            top1_idx = jnp.argmax(expert_scores + exp_bias, axis=-1)
            top1_score = jnp.take_along_axis(expert_scores, top1_idx[:, None], axis=-1)
            weights = jax.nn.softmax(jnp.concatenate([shared_scores, top1_score], axis=-1), axis=-1)
            shared_w, expert_w = (weights[:, 0], weights[:, 1])
            shared_moe_out = shared_out[index_b, index_t] * shared_w[:, None]
            h1 = jnp.einsum('md,ehd->meh', x_moe, ew1) + eb1
            h2 = jnp.einsum('md,ehd->meh', x_moe, ew2) + eb2
            z = _ln(jax.nn.silu(h1) * h2, sel_ln_g, sel_ln_b)
            out_all = jnp.einsum('meh,edh->med', z, ew3) + eb3
            expert_out = jnp.take_along_axis(out_all, top1_idx[:, None, None], axis=1)[:, 0]
            expert_moe_out = expert_out * expert_w[:, None]
            final_out = shared_out.at[index_b, index_t].set(shared_moe_out + expert_moe_out)
            return final_out
        return _forward(x, index_b, index_t, sw1, sb1, sw2, sb2, sw3, sb3, s_ln_g, s_ln_b, sg_w, sg_b, eg_w, eg_b, exp_bias, ew1, eb1, ew2, eb2, ew3, eb3, sel_ln_g, sel_ln_b)
    x = x + _L0_attn_ref(_layernorm(x, axis=-1), L0_attn_w_qkv, L0_attn_w_out)
    x = x + _L0_xattn_ref(_layernorm(x, axis=-1), ctx_1024, ctx_1024, mask_BxS2_bf0, L0_xattn_Wq, L0_xattn_bq, L0_xattn_Wk, L0_xattn_bk, L0_xattn_Wv, L0_xattn_bv, L0_xattn_Wo, L0_xattn_bo)
    x = x + _L0_ffn_ref(_layernorm(x, axis=-1), L0_ffn_index_b, L0_ffn_index_t, L0_ffn_sw1, L0_ffn_sb1, L0_ffn_sw2, L0_ffn_sb2, L0_ffn_sw3, L0_ffn_sb3, L0_ffn_s_ln_g, L0_ffn_s_ln_b, L0_ffn_sg_w, L0_ffn_sg_b, L0_ffn_eg_w, L0_ffn_eg_b, L0_ffn_exp_bias, L0_ffn_ew1, L0_ffn_eb1, L0_ffn_ew2, L0_ffn_eb2, L0_ffn_ew3, L0_ffn_eb3, L0_ffn_sel_ln_g, L0_ffn_sel_ln_b)
    return x

_drawn_inputs = setup_inputs


def setup_inputs(seed=0):
    import zlib

    import numpy as np

    out = dict(_drawn_inputs(seed))
    spreads = {'L0_xattn_bq': (0.0, 0.345),
     'L0_xattn_bk': (0.0, 2.0),
     'L0_xattn_bv': (0.0, 0.1),
     'L0_xattn_bo': (0.0, 0.1),
     'L0_ffn_sb1': (0.0, 0.277),
     'L0_ffn_sb2': (0.0, 0.1),
     'L0_ffn_sb3': (0.0, 0.1),
     'L0_ffn_s_ln_g': (1.0, 0.567),
     'L0_ffn_s_ln_b': (0.0, 0.333),
     'L0_ffn_eg_b': (0.0, 0.281),
     'L0_ffn_exp_bias': (0.0, 0.1),
     'L0_ffn_eb1': (0.0, 0.482),
     'L0_ffn_eb2': (0.0, 0.466),
     'L0_ffn_eb3': (0.0, 0.367),
     'L0_ffn_sel_ln_g': (1.0, 0.6),
     'L0_ffn_sel_ln_b': (0.0, 0.8)}
    factors = {'L0_attn_w_qkv': 4.072, 'L0_attn_w_out': 3.137, 'L0_ffn_sg_w': 26.846}
    for name, (base, spread) in spreads.items():
        noise = np.random.default_rng([zlib.crc32(name.encode()), seed]).standard_normal(out[name].shape)
        drawn = base * np.exp(spread * noise) if base else spread * noise
        out[name] = jnp.asarray(drawn.astype(out[name].dtype))
    for name, factor in factors.items():
        out[name] = (out[name] * factor).astype(out[name].dtype)
    return out
```

```python
from contextlib import ExitStack

import concourse.bass as bass
from concourse import mybir

ALU = mybir.AluOpType
ACT = mybir.ActivationFunctionType
AX = mybir.AxisListType
F32 = mybir.dt.float32
F32R = mybir.dt.float32r
BF16 = mybir.dt.bfloat16
I32 = mybir.dt.int32

P = 128
B, S, D = 2, 2048, 512
H, HD = 16, 32
DC = D // P
BLK = 512
TPB = BLK // P
NBLK = B * S // BLK
BPB = S // BLK
EPS = 1e-5


U8 = mybir.dt.uint8
SC = 154
KH = SC // 2
MASKED = -2.0 ** 127
HF = 256
HC = HF // P
E = 8
M = 1024


def stage_semaphores(nc, ctx, prefix):
    taken = []

    def sem(name):
        taken.append(nc.alloc_semaphore(prefix + name))
        return taken[-1]

    def give_back():
        nc.clear_and_free_semaphores(taken)
        nc.all_engine_barrier()

    ctx.callback(give_back)
    return sem
def project_qkv(nc, x_rows, wqk_t, wv_t, eye, q_hi, q_lo, k_hi, k_lo, v_rows):
    with ExitStack() as ctx:
        sb = lambda name, shape, dt=F32: ctx.enter_context(nc.sbuf_tensor(name, shape, dt))
        sem = stage_semaphores(nc, ctx, "a_")
        QK = 2 * D // P
        wqk_raw = sb("wqk_raw", [P, DC, 2 * D])
        wv_raw = sb("wv_raw", [P, DC, D])
        wqk_h = sb("wqk_h", [P, DC, 2 * D], F32R)
        wqk_l = sb("wqk_l", [P, DC, 2 * D], F32R)
        wv_h = sb("wv_h", [P, DC, D], F32R)
        wv_l = sb("wv_l", [P, DC, D], F32R)
        ident = sb("identity", [P, P])
        x_in = sb("x_in", [P, 2, TPB, D])
        x_norm = sb("x_norm", [P, TPB, D])
        xt_h = sb("xt_h", [P, 2, DC, BLK], F32R)
        xt_l = sb("xt_l", [P, 2, DC, BLK], F32R)
        stats = sb("stats", [P, TPB, 6])
        moments = sb("moments", [P, TPB, 2])
        var_eps = sb("var_eps", [P, TPB])
        minus_half = sb("minus_half", [P, TPB])
        rstd = sb("rstd", [P, TPB])
        qk_h_out = sb("qk_h_out", [P, QK, BLK], F32R)
        qk_l_out = sb("qk_l_out", [P, QK, BLK], F32R)
        v_out = sb("v_out", [P, TPB, H // 2, 3 * HD])
        ps_t = ctx.enter_context(nc.psum_tensor("ps_t", [P, 2, DC, P], F32))
        ps_g = ctx.enter_context(nc.psum_tensor("ps_g", [P, 4, BLK], F32))
        GROUPS = QK + TPB

        w_loaded, w_high, w_low = sem("w_loaded"), sem("w_high"), sem("w_low")
        x_loaded = [sem(f"x_loaded{s}") for s in range(2)]
        consts, v_ones_set = sem("consts"), sem("v_ones_set")
        stats_done, moments_done, eps_added = sem("stats_done"), sem("moments_done"), sem("eps_added")
        rstd_done, normed, xt_in_psum = sem("rstd_done"), sem("normed"), sem("xt_in_psum")
        xt_high, xt_low = sem("xt_high"), sem("xt_low")
        group_done, group_high, group_low = sem("group_done"), sem("group_high"), sem("group_low")
        stored = {n: sem(f"stored_{n}") for n in ("q_hi", "q_lo", "k_hi", "k_lo", "v")}

        x_blocks = x_rows.rearrange("(n t p) d -> n p t d", t=TPB, p=P)
        v_blocks = v_rows.rearrange("(n t p) r c -> n p t (r c)", t=TPB, p=P)

        def blocks(engine, body):
            body(0, 0, False)
            body(0, 1, False)
            with engine.Fori(1, NBLK // 2 - 1) as i:
                body(i, 0, False)
                body(i, 1, False)
            body(NBLK // 2 - 1, 0, False)
            body(NBLK // 2 - 1, 1, True)

        def first(i, u):
            return isinstance(i, int) and i == 0 and u == 0

        def count(i, u, per, c):
            return i * (2 * per) + (u * per + c)

        stats_seen = sem("stats_seen")
        with nc.Block() as block:

            @block.sync
            def _(sp):
                sp.dma_start(ident[:], eye).then_inc(w_loaded, 16)
                sp.dma_start(wqk_raw[:], wqk_t.rearrange("(c p) n -> p c n", p=P)).then_inc(w_loaded, 16)
                sp.dma_start(wv_raw[:], wv_t.rearrange("(c p) n -> p c n", p=P)).then_inc(w_loaded, 16)

                def body(i, u, last):
                    q_block = 2 * i + u
                    if not (isinstance(i, int) and i == NBLK // 2 - 1):
                        sp.wait_ge(normed, count(i, u, TPB, TPB))
                        sp.dma_start(x_in[:, u], x_blocks[q_block + 2]).then_inc(x_loaded[u], 16)
                    for part, (name_h, name_l) in enumerate((("q_hi", "q_lo"), ("k_hi", "k_lo"))):
                        c0 = part * DC
                        sp.wait_ge(group_high, count(i, u, GROUPS, c0 + DC))
                        sp.dma_start(feat_at(name_h, i, u), qk_h_out[:, c0:c0 + DC].bitcast(F32)).then_inc(stored[name_h], 16)
                        sp.wait_ge(group_low, count(i, u, QK, c0 + DC))
                        sp.dma_start(feat_at(name_l, i, u), qk_l_out[:, c0:c0 + DC].bitcast(F32)).then_inc(stored[name_l], 16)
                    sp.wait_ge(group_high, count(i, u, GROUPS, GROUPS))
                    sp.dma_start(v_blocks[q_block], v_out[:].rearrange("p t r c -> p t (r c)")).then_inc(stored["v"], 16)

                scratch = {"q_hi": q_hi, "q_lo": q_lo, "k_hi": k_hi, "k_lo": k_lo}

                def feat_at(name, i, u):
                    n = 2 * i + u
                    return scratch[name].rearrange("b (c p) (n k) -> b n p c k", p=P, k=BLK)[n // BPB, n % BPB]

                for s in range(2):
                    sp.dma_start(x_in[:, s], x_blocks[s]).then_inc(x_loaded[s], 16)
                blocks(sp, body)
                for name in stored:
                    sp.wait_ge(stored[name], 16 * NBLK)

            @block.gpsimd
            def _(pool):
                pool.memset(minus_half[:], -0.5).then_inc(consts, 1)
                pool.memset(v_out[:, :, :, HD:2 * HD], 1.0).then_inc(v_ones_set, 1)
                pool.wait_ge(consts, 1)
                with pool.Fori(0, NBLK) as n:
                    pool.wait_ge(eps_added, n + 1)
                    pool.tensor_tensor(rstd[:], var_eps[:], minus_half[:], ALU.pow).then_inc(rstd_done, 1)

            @block.vector
            def _(dve):
                dve.wait_ge(w_loaded, 48)
                dve.tensor_copy(wqk_h[:], wqk_raw[:]).then_inc(w_high, 1)
                dve.tensor_copy(wv_h[:], wv_raw[:]).then_inc(w_high, 1)
                dve.wait_ge(w_high, 2)
                dve.tensor_tensor(wqk_l[:], wqk_raw[:], wqk_h[:].bitcast(F32), ALU.subtract).then_inc(w_low, 1)
                dve.tensor_tensor(wv_l[:], wv_raw[:], wv_h[:].bitcast(F32), ALU.subtract).then_inc(w_low, 1)

                def norm(i, u):
                    dve.wait_ge(x_loaded[u], i * 16 + 16)
                    for t in range(TPB):
                        dve.bn_stats(stats[:, t], x_in[:, u, t]).then_inc(stats_done, 1)
                    dve.wait_ge(stats_done, count(i, u, TPB, TPB))
                    dve.sem_inc(stats_seen, 1)
                    for t in range(TPB):
                        dve.bn_aggr(moments[:, t], stats[:, t]).then_inc(moments_done, 1)
                    dve.wait_ge(moments_done, count(i, u, TPB, TPB))
                    dve.tensor_scalar(var_eps[:], moments[:, :, 1], EPS, None, ALU.add).then_inc(eps_added, 1)
                    dve.wait_ge(rstd_done, count(i, u, 1, 1))
                    if not first(i, u):
                        dve.wait_ge(xt_in_psum, count(i, u, TPB, 0))
                    for t in range(TPB):
                        dve.tensor_scalar(x_norm[:, t], x_in[:, u, t], moments[:, t, 0:1], rstd[:, t:t + 1],
                                          ALU.subtract, ALU.mult).then_inc(normed, 1)

                def transposed(i, u):
                    for t in range(TPB):
                        dve.wait_ge(xt_high, count(i, u, TPB, t + 1))
                        dve.tensor_tensor(xt_l[:, u, :, t * P:(t + 1) * P], ps_t[:, t % 2],
                                          xt_h[:, u, :, t * P:(t + 1) * P].bitcast(F32),
                                          ALU.subtract).then_inc(xt_low, 1)

                def group(i, u, g):
                    dve.wait_ge(group_high, count(i, u, GROUPS, g + 1))
                    if g % DC == 0 and not first(i, u):
                        dve.wait_ge(stored["q_lo" if g == 0 else "k_lo"], count(i, u, 16, 0))
                    dve.tensor_tensor(qk_l_out[:, g], ps_g[:, g % 4], qk_h_out[:, g].bitcast(F32),
                                      ALU.subtract).then_inc(group_low, 1)

                def body(i, u, last):
                    if not last:
                        norm(i + u, 1 - u)
                    for g in range(QK // 2):
                        group(i, u, g)
                    if not last:
                        transposed(i + u, 1 - u)
                    for g in range(QK // 2, QK):
                        group(i, u, g)

                norm(0, 0)
                transposed(0, 0)
                blocks(dve, body)

            @block.scalar
            def _(act):
                def transposed(i, u):
                    for t in range(TPB):
                        act.wait_ge(xt_in_psum, count(i, u, TPB, t + 1))
                        act.activation(xt_h[:, u, :, t * P:(t + 1) * P], ps_t[:, t % 2], ACT.Copy).then_inc(xt_high, 1)

                def group(i, u, g):
                    act.wait_ge(group_done, count(i, u, GROUPS, g + 1))
                    if g < QK:
                        if g % DC == 0 and not first(i, u):
                            act.wait_ge(stored["q_hi" if g == 0 else "k_hi"], count(i, u, 16, 0))
                        out = qk_h_out[:, g]
                    else:
                        if g == QK:
                            if first(i, u):
                                act.wait_ge(v_ones_set, 1)
                            else:
                                act.wait_ge(stored["v"], count(i, u, 16, 0))
                        out = v_out[:, g - QK].rearrange("p r (a c) -> p r a c", c=HD)[:, :, 0::2]
                    src = ps_g[:, g % 4] if g < QK else ps_g[:, g % 4].rearrange("p (r a c) -> p r a c", a=2, c=HD)
                    act.activation(out, src, ACT.Copy).then_inc(group_high, 1)

                def body(i, u, last):
                    for g in range(GROUPS):
                        if g == GROUPS // 2 and not last:
                            transposed(i + u, 1 - u)
                        group(i, u, g)

                transposed(0, 0)
                blocks(act, body)

            @block.tensor
            def _(pe):
                def transposes(i, u):
                    for t in range(TPB):
                        pe.wait_ge(normed, count(i, u, TPB, t + 1))
                        if not (first(i, u) and t < 2):
                            pe.wait_ge(xt_low, count(i, u, TPB, t - 1))
                        for c in range(DC):
                            mm = pe.transpose(ps_t[:, t % 2, c], x_norm[:, t, c * P:(c + 1) * P], ident[:])
                        mm.then_inc(xt_in_psum, 1)

                def group(i, u, g):
                    if g >= 4:
                        pe.wait_ge(group_high, count(i, u, GROUPS, g - 3))
                        pe.wait_ge(group_low, count(i, u, QK, g - 3))
                    elif not first(i, u):
                        pe.wait_ge(group_high, count(i, u, GROUPS, g - 3))
                    parts = ((0, 0), (0, 1), (1, 0))
                    xt, wqk, wv = (xt_h, xt_l), (wqk_h, wqk_l), (wv_h, wv_l)
                    n = 0
                    for a, b in parts:
                        for c in range(DC):
                            if g < QK:
                                lhs, rhs = wqk[b][:, c, g * P:(g + 1) * P], xt[a][:, u, c]
                            else:
                                t = g - QK
                                lhs, rhs = xt[a][:, u, c, t * P:(t + 1) * P], wv[b][:, c]
                            mm = pe.matmul(ps_g[:, g % 4], lhs, rhs, start=(n == 0), stop=(n == 3 * DC - 1))
                            n += 1
                    mm.then_inc(group_done, 1)

                def body(i, u, last):
                    pe.wait_ge(xt_low, count(i, u, TPB, TPB))
                    for g in range(GROUPS):
                        if g == GROUPS // 2 and not last:
                            transposes(i + u, 1 - u)
                        group(i, u, g)

                pe.wait_ge(w_low, 2)
                transposes(0, 0)
                blocks(pe, body)
def self_attention(nc, q_hi, q_lo, k_hi, k_lo, v_rows, eye_bf, attn_t, sums):
    PAIRS = H // 2
    KT = S // P
    UNITS = B * PAIRS * BPB
    UPB = 2 * BPB
    ROWS = 3 * HD
    TOP = ROWS + 3
    SLOTS = 2 * TPB * 2
    SLOTS_AT = [1, 1, 1, 1, 1, 1, 1, 1, 2, 1, 1, 2, 1, 1, 0, 0]
    MAX_AT = 15
    SCALE = float(HD) ** -0.5
    with ExitStack() as ctx:
        sb = lambda name, shape, dt=F32: ctx.enter_context(nc.sbuf_tensor(name, shape, dt))
        sem = stage_semaphores(nc, ctx, "b_")
        k_stack = sb("k_stack", [TOP, 2, 2, S], F32R)
        q_stack = sb("q_stack", [TOP, 4, 2, BLK], F32R)
        v_ones = sb("v_ones", [P, 2, KT, 3 * HD])
        probs = sb("probs", [P, 4, 2, BLK])
        part_max = sb("part_max", [P, SLOTS])
        neg_max = sb("neg_max", [P, SLOTS // 2])
        rest = sb("rest", [P, 2, SLOTS // 2])
        max_parts = sb("max_parts", [P, SLOTS // 2, 3], BF16)
        ident_bf = sb("ident_bf", [P, P], BF16)
        attn_out = sb("attn_out", [P, 2, BLK])
        ps_st = ctx.enter_context(nc.psum_tensor("ps_st", [P, 2, BLK], F32))
        ps_s = ctx.enter_context(nc.psum_tensor("ps_s", [P, 2, 2, BLK], F32))
        ps_pv = ctx.enter_context(nc.psum_tensor("ps_pv", [P, 2, BLK], F32))

        q_loaded = [sem(f"q_loaded{s}") for s in range(4)]
        k_loaded = [sem(f"k_loaded{s}") for s in range(2)]
        v_loaded = [sem(f"v_loaded{s}") for s in range(2)]
        ident_loaded, ones_set = sem("ident_loaded"), sem("ones_set")
        scores_done, max_done, chain = sem("scores_done"), sem("max_done"), sem("max_chain")
        parts_done, max_turned, max_rows_done = sem("parts_done"), sem("max_turned"), sem("max_rows_done")
        st_done, exp_done, pv_done = sem("st_done"), sem("exp_done"), sem("pv_done")
        out_done = sem("out_done")
        out_stored = [sem(f"out_stored{s}") for s in range(2)]
        ST_FREE, PROBS_FREE, PV_FREE = 2, 4, 2
        CHAIN = 5
        OUT_DMAS = 3

        def at(i, w, per, c):
            return i * (UPB * per) + (w * per + c)

        def after(i, w):
            return (i + 1, 0) if w == UPB - 1 else (i, w + 1)

        def slots_of():
            s = 0
            for n in SLOTS_AT:
                yield range(s, s + n)
                s += n
            assert s == SLOTS

        SLOTS_OF = list(slots_of())

        q_units = [s.rearrange("b (p j r) (n k) -> b p n r j k", p=PAIRS, j=2, n=BPB) for s in (q_hi, q_lo)]
        k_pairs = [s.rearrange("b (p j r) k -> b p r j k", p=PAIRS, j=2) for s in (k_hi, k_lo)]
        v_pairs = v_rows.rearrange("(b t q) p c -> b p q t c", b=B, q=P)
        out_units = attn_t.rearrange("b (p j c) (n k) -> b p n j c k", p=PAIRS, j=2, n=BPB)
        sum_units = sums.rearrange("(u j) k -> u j k", j=2)

        with nc.Block() as block:

            @block.sync
            def _(sp):
                def load_q(unit, buf):
                    b, p, n = unit // (PAIRS * BPB), unit % (PAIRS * BPB) // BPB, buf
                    for row, part in ((0, 0), (1, 1), (2, 0)):
                        sp.dma_start(q_stack[row * HD:(row + 1) * HD, buf].bitcast(F32),
                                     q_units[part][b, p, n]).then_inc(q_loaded[buf], 16)

                def load_k(pair, buf):
                    b, p = pair // PAIRS, pair % PAIRS
                    for row, part in ((0, 0), (1, 0), (2, 1)):
                        sp.dma_start(k_stack[row * HD:(row + 1) * HD, buf].bitcast(F32),
                                     k_pairs[part][b, p]).then_inc(k_loaded[buf], 16)

                def load_v(pair, buf):
                    b, p = pair // PAIRS, pair % PAIRS
                    sp.dma_start(v_ones[:, buf], v_pairs[b, p]).then_inc(v_loaded[buf], 16)

                def body(i, last):
                    for w in range(UPB):
                        if not last or w <= BPB:
                            sp.wait_ge(st_done, at(i, w, 2 * KT, 2 * KT))
                            load_q((i * UPB + (w + 4)) % UNITS, w % 4)
                        if w % BPB == BPB - 1:
                            c = w // BPB
                            if not last or c == 0:
                                sp.wait_ge(st_done, at(i, w, 2 * KT, 2 * KT))
                                load_k((i * 2 + (c + 2)) % (UNITS // BPB), c)
                            if not last:
                                sp.wait_ge(pv_done, at(i, w, KT, KT) + PROBS_FREE)
                                load_v((i * 2 + (c + 2)) % (UNITS // BPB), c)
                        sp.wait_ge(out_done, at(i, w, 1, 1) + PV_FREE)
                        pair, n = i * 2 + w // BPB, w % BPB
                        b, p = pair // PAIRS, pair % PAIRS
                        for j, row in ((0, 0), (1, 3 * HD)):
                            sp.dma_start(out_units[b, p, n, j], attn_out[row:row + HD, w % 2])\
                              .then_inc(out_stored[w % 2], 16)
                        sp.dma_start(sum_units[pair, :, n * BLK:(n + 1) * BLK], attn_out[HD:3 * HD:HD, w % 2])\
                          .then_inc(out_stored[w % 2], 16)

                sp.dma_start(ident_bf[:], eye_bf).then_inc(ident_loaded, 16)
                load_k(0, 0)
                for u in range(4):
                    load_q(u, u)
                load_v(0, 0)
                load_k(1, 1)
                load_v(1, 1)
                with sp.Fori(0, UNITS // UPB - 1) as i:
                    body(i, False)
                body(UNITS // UPB - 1, True)
                for s in range(2):
                    sp.wait_ge(out_stored[s], OUT_DMAS * 16 * UNITS // 2)

            @block.gpsimd
            def _(pool):
                pool.memset(k_stack[ROWS:TOP, :, :, :].bitcast(F32), 1.0).then_inc(ones_set, 1)

            @block.tensor
            def _(pe):
                def scores(i, w, s):
                    j, t, half = s // (2 * TPB), s % (2 * TPB) // 2, s % 2
                    if s == 0:
                        pe.wait_ge(max_done, at(i, w, SLOTS, 0))
                        pe.wait_ge(q_loaded[w % 4], i * (2 * 48) + 48 * (w // 4 + 1))
                        pe.wait_ge(k_loaded[w // BPB], i * 48 + 48)
                    elif s == 1:
                        pe.wait_ge(max_rows_done, at(i, w, 1, 0))
                    else:
                        pe.wait_ge(max_done, at(i, w, SLOTS, s - 1))
                    for n in range(2):
                        k0 = (2 * half + n) * BLK
                        mm = pe.matmul(ps_s[:, (w + s) % 2, n], q_stack[0:ROWS, w % 4, j, t * P:(t + 1) * P],
                                       k_stack[0:ROWS, w // BPB, j, k0:k0 + BLK], start=True, stop=True)
                    mm.then_inc(scores_done, 1)

                def turn_max(i, w):
                    pe.wait_ge(parts_done, at(i, w, 1, 1))
                    for j in range(2):
                        for t in range(TPB):
                            mm = pe.matmul(ps_s[ROWS:TOP, (w + SLOTS) % 2, j, t * P:(t + 1) * P],
                                           max_parts[:, j * TPB + t, :], ident_bf[:], start=True, stop=True)
                    mm.then_inc(max_turned, 1)

                def transposed_scores(i, w, k):
                    for j in range(2):
                        pe.wait_ge(exp_done, at(i, w, 2 * KT, 2 * k + j - 1) + ST_FREE)
                        pe.matmul(ps_st[:, j], k_stack[:, w // BPB, j, k * P:(k + 1) * P],
                                  q_stack[:, w % 4, j, :], start=True, stop=True).then_inc(st_done, 1)

                def weighted_values(i, w, k):
                    if k == 0:
                        pe.wait_ge(v_loaded[w // BPB], i * 16 + 16)
                        pe.wait_ge(out_done, at(i, w, 1, 1))
                    pe.wait_ge(exp_done, at(i, w, 2 * KT, 2 * k + 2) + ST_FREE)
                    for j in range(2):
                        mm = pe.matmul(ps_pv[j * 2 * HD:(j + 1) * 2 * HD, w % 2],
                                       v_ones[:, w // BPB, k, j * HD:(j + 2) * HD], probs[:, k % 4, j],
                                       start=(k == 0), stop=(k == KT - 1))
                    mm.then_inc(pv_done, 1)

                pe.sem_inc(pv_done, PROBS_FREE)
                pe.wait_ge(ones_set, 1)
                pe.wait_ge(ident_loaded, 16)
                for s in range(SLOTS):
                    scores(0, 0, s)
                turn_max(0, 0)
                with pe.Fori(0, UNITS // UPB) as i:
                    for w in range(UPB):
                        i2, w2 = after(i, w)
                        pe.wait_ge(max_rows_done, at(i, w, 1, 1))
                        for k in range(KT):
                            transposed_scores(i, w, k)
                            if k:
                                weighted_values(i, w, k - 1)
                            for s in SLOTS_OF[k]:
                                scores(i2, w2, s)
                            if k == MAX_AT:
                                turn_max(i2, w2)
                        weighted_values(i, w, KT - 1)

            @block.vector
            def _(dve):
                def slot_max(i, w, s):
                    dve.wait_ge(scores_done, at(i, w, SLOTS, s + 1))
                    dve.tensor_reduce(part_max[:, s:s + 1], ps_s[:, (w + s) % 2], AX.XY, ALU.max).then_inc(max_done, 1)

                def max_rows(i, w):
                    dve.wait_ge(max_done, at(i, w, SLOTS, SLOTS))
                    dve.tensor_reduce(neg_max[:], part_max[:].rearrange("p (t h) -> p t h", h=2), AX.X,
                                      ALU.max, negate=True).then_inc(chain, 1)
                    left = neg_max[:]
                    for n in range(2):
                        dve.wait_ge(chain, at(i, w, CHAIN, 2 * n + 1))
                        dve.tensor_copy(max_parts[:, :, n], left).then_inc(chain, 1)
                        dve.wait_ge(chain, at(i, w, CHAIN, 2 * n + 2))
                        dve.tensor_tensor(rest[:, n], left, max_parts[:, :, n], ALU.subtract).then_inc(chain, 1)
                        left = rest[:, n]
                    dve.wait_ge(chain, at(i, w, CHAIN, CHAIN))
                    dve.tensor_copy(max_parts[:, :, 2], left).then_inc(parts_done, 1)
                    dve.wait_ge(max_turned, at(i, w, 1, 1))
                    dve.tensor_copy(q_stack[ROWS:TOP, w % 4], ps_s[ROWS:TOP, (w + SLOTS) % 2]).then_inc(max_rows_done, 1)

                for s in range(SLOTS):
                    slot_max(0, 0, s)
                max_rows(0, 0)
                with dve.Fori(0, UNITS // UPB) as i:
                    for w in range(UPB):
                        i2, w2 = after(i, w)
                        for s in range(SLOTS):
                            slot_max(i2, w2, s)
                        max_rows(i2, w2)

            @block.scalar
            def _(act):
                act.sem_inc(exp_done, ST_FREE)
                act.sem_inc(out_done, PV_FREE)
                with act.Fori(0, UNITS // UPB) as i:
                    for w in range(UPB):
                        for k in range(KT):
                            act.wait_ge(pv_done, at(i, w, KT, k - 3) + PROBS_FREE)
                            for j in range(2):
                                act.wait_ge(st_done, at(i, w, 2 * KT, 2 * k + j + 1))
                                act.activation(probs[:, k % 4, j], ps_st[:, j], ACT.Exp, scale=SCALE).then_inc(exp_done, 1)
                        act.wait_ge(out_stored[w % 2], i * (OUT_DMAS * 16 * UPB // 2) + OUT_DMAS * 16 * (w // 2))
                        act.wait_ge(pv_done, at(i, w, KT, KT) + PROBS_FREE)
                        act.activation(attn_out[:, w % 2], ps_pv[:, w % 2], ACT.Copy).then_inc(out_done, 1)


def attention_to_queries(nc, x_rows, attn_t, sums, inv_sums, wo_t, wq_t, bq_cols, eye, x1_rows, q_parts):
    with ExitStack() as ctx:
        sb = lambda name, shape, dt=F32: ctx.enter_context(nc.sbuf_tensor(name, shape, dt))
        sem = stage_semaphores(nc, ctx, "c_")
        w_raw = sb("c_w_raw", [P, 2, DC, D])
        w_h = sb("c_w_h", [P, 2, DC, D], F32R)
        w_l = sb("c_w_l", [P, 2, DC, D], F32R)
        bq_sb = sb("bq_sb", [P, DC])
        ident = sb("c_identity", [P, P])
        sums_sb = sb("sums_sb", [P, BLK])
        inv_sb = sb("inv_sb", [P, BLK])
        a_raw = sb("a_raw", [P, 2, DC, BLK])
        a_inv = sb("a_inv", [P, 2, DC, BLK])
        a_norm = sb("a_norm", [P, DC, BLK])
        a_h = sb("a_h", [P, DC, BLK], F32R)
        a_l = sb("a_l", [P, DC, BLK], F32R)
        x_in = sb("c_x_in", [P, 2, TPB, D])
        x1 = sb("x1", [P, 2, TPB, D])
        x_norm = sb("c_x_norm", [P, TPB, D])
        xt_h = sb("c_xt_h", [P, 2, DC, BLK], F32R)
        xt_l = sb("c_xt_l", [P, 2, DC, BLK], F32R)
        stats = sb("c_stats", [P, TPB, 6])
        moments = sb("c_moments", [P, TPB, 2])
        var_eps = sb("c_var_eps", [P, TPB])
        minus_half = sb("c_minus_half", [P, TPB])
        rstd = sb("c_rstd", [P, TPB])
        q_h = sb("q_h_out", [P, DC, BLK], F32R)
        q_l = sb("q_l_out", [P, DC, BLK], F32R)
        ps_t = ctx.enter_context(nc.psum_tensor("c_ps_t", [P, 2, DC, P], F32))
        ps_g = ctx.enter_context(nc.psum_tensor("c_ps_g", [P, 4, BLK], F32))
        ps_p = ctx.enter_context(nc.psum_tensor("c_ps_p", [P, 2, D], F32))

        w_loaded, w_high, w_low, consts = (sem(f"c_{n}") for n in ("w_loaded", "w_high", "w_low", "consts"))
        sums_loaded, inv_made, inv_stored = (sem(n) for n in ("sums_loaded", "inv_made", "inv_stored"))
        loaded = [sem(f"c_block_loaded{s}") for s in range(2)]
        LOADS = 2 + DC
        scaled, a_high, a_low = sem("a_scaled"), sem("a_high"), sem("a_low")
        proj_done, resid_done = sem("c_proj_done"), sem("c_resid_done")
        stats_done, moments_done, eps_added, rstd_done, normed, xt_in_psum, xt_high, xt_low = (
            sem(f"c_{n}") for n in ("stats_done", "moments_done", "eps_added", "rstd_done", "normed", "xt_in_psum",
                                    "xt_high", "xt_low"))
        group_done, group_high, group_low = (sem(f"c_{n}") for n in ("group_done", "group_high", "group_low"))
        q_stored = sem("q_stored")
        x1_stored = [sem(f"x1_stored{s}") for s in range(2)]
        Q_DMAS = 3 * (P // HD)

        x_blocks = x_rows.rearrange("(n t p) d -> n p t d", t=TPB, p=P)
        x1_blocks = x1_rows.rearrange("(n t p) d -> n p t d", t=TPB, p=P)
        a_blocks = attn_t.rearrange("b (c p) (n k) -> b n p c k", p=P, k=BLK)
        inv_blocks = inv_sums.rearrange("(b c g) (n k) -> b n c g k", b=B, c=DC, k=BLK)
        q_blocks = q_parts.rearrange("n (c h) (s r) j k -> n s h j r c k", h=2, s=3)

        def first(i, u):
            return isinstance(i, int) and i == 0 and u == 0

        def final_pair(i):
            return isinstance(i, int) and i == NBLK // 2 - 1

        def count(i, u, per, c):
            return i * (2 * per) + (u * per + c)

        def blocks(engine, body):
            body(0, 0, False)
            body(0, 1, False)
            with engine.Fori(1, NBLK // 2 - 1) as i:
                body(i, 0, False)
                body(i, 1, False)
            body(NBLK // 2 - 1, 0, False)
            body(NBLK // 2 - 1, 1, True)

        stats_seen = sem("stats_seen")
        with nc.Block() as block:

            @block.sync
            def _(sp):
                def load(n, slot):
                    b, k = n // BPB, n % BPB
                    sp.dma_start(a_raw[:, slot], a_blocks[b, k]).then_inc(loaded[slot], 16)
                    for c in range(DC):
                        src = inv_blocks[b, k, c].unsqueeze(1).to_broadcast([P // HD, HD, BLK])
                        sp.dma_start(a_inv[:, slot, c], src).then_inc(loaded[slot], 16)
                    sp.dma_start(x_in[:, slot], x_blocks[n]).then_inc(loaded[slot], 16)

                sp.dma_start(sums_sb[:], sums.rearrange("h (n k) -> (h n) k", k=BLK)).then_inc(sums_loaded, 16)
                rows = lambda w: w.rearrange("(c p) n -> p c n", p=P)
                sp.dma_start(ident[:], eye).then_inc(w_loaded, 16)
                sp.dma_start(w_raw[:, 0], rows(wo_t)).then_inc(w_loaded, 16)
                sp.dma_start(w_raw[:, 1], rows(wq_t)).then_inc(w_loaded, 16)
                sp.dma_start(bq_sb[:], bq_cols).then_inc(w_loaded, 16)
                sp.wait_ge(inv_made, 1)
                sp.dma_start(inv_sums.rearrange("h (n k) -> (h n) k", k=BLK), inv_sb[:]).then_inc(inv_stored, 16)
                sp.wait_ge(inv_stored, 16)
                load(0, 0)
                load(1, 1)
                def store_x1(i, u):
                    sp.wait_ge(resid_done, count(i, u, TPB, TPB))
                    sp.dma_start(x1_blocks[2 * i + u], x1[:, u]).then_inc(x1_stored[u], 16)

                store_x1(0, 0)
                load(2, 0)

                def body(i, u, last):
                    if not last:
                        i2, u2 = (i, 1) if u == 0 else (i + 1, 0)
                        store_x1(i2, u2)
                        if not (final_pair(i) or (isinstance(i, int) and i == NBLK // 2 - 2 and u == 1)):
                            load(2 * i2 + (u2 + 2), u2)
                    sp.wait_ge(group_high, count(i, u, DC, DC))
                    sp.wait_ge(group_low, count(i, u, DC, DC))
                    for h in range(2):
                        for j in range(2):
                            r = (2 * h + j) * HD
                            for s, src in enumerate((q_h, q_l, q_h)):
                                sp.dma_start(q_blocks[2 * i + u][s, h, j], src[r:r + HD].bitcast(F32)).then_inc(q_stored, 16)

                body(0, 0, False)
                body(0, 1, False)
                with sp.Fori(1, NBLK // 2 - 2) as i:
                    body(i, 0, False)
                    body(i, 1, False)
                for i in range(NBLK // 2 - 2, NBLK // 2):
                    body(i, 0, False)
                    body(i, 1, i == NBLK // 2 - 1)
                for s in range(2):
                    sp.wait_ge(x1_stored[s], 16 * NBLK // 2)
                sp.wait_ge(q_stored, 16 * Q_DMAS * NBLK)

            @block.gpsimd
            def _(pool):
                def scale(i, u):
                    pool.wait_ge(loaded[u], i * (16 * LOADS) + 16 * LOADS)
                    if not first(i, u):
                        pool.wait_ge(a_low, count(i, u, 1, 0))
                    pool.tensor_tensor(a_norm[:], a_raw[:, u], a_inv[:, u], ALU.mult).then_inc(scaled, 1)

                def rsqrt(i, u):
                    pool.wait_ge(eps_added, count(i, u, 1, 1))
                    pool.tensor_tensor(rstd[:], var_eps[:], minus_half[:], ALU.pow).then_inc(rstd_done, 1)

                def body(i, u, last):
                    if not last:
                        if not final_pair(i):
                            scale(i + 1, u)
                        rsqrt(*((i, 1) if u == 0 else (i + 1, 0)))

                pool.memset(minus_half[:], -0.5).then_inc(consts, 1)
                scale(0, 0)
                pool.wait_ge(consts, 1)
                scale(0, 1)
                rsqrt(0, 0)
                blocks(pool, body)

            @block.vector
            def _(dve):
                dve.wait_ge(sums_loaded, 16)
                dve.reciprocal(inv_sb[:], sums_sb[:]).then_inc(inv_made, 1)
                dve.wait_ge(w_loaded, 64)
                for n in range(2):
                    dve.tensor_copy(w_h[:, n], w_raw[:, n]).then_inc(w_high, 1)
                for n in range(2):
                    dve.wait_ge(w_high, n + 1)
                    dve.tensor_tensor(w_l[:, n], w_raw[:, n], w_h[:, n].bitcast(F32), ALU.subtract).then_inc(w_low, 1)

                def split(i, u):
                    dve.wait_ge(a_high, count(i, u, 1, 1))
                    if not first(i, u):
                        dve.wait_ge(proj_done, count(i, u, TPB, 0))
                    dve.tensor_tensor(a_l[:], a_norm[:], a_h[:].bitcast(F32), ALU.subtract).then_inc(a_low, 1)

                def residual(i, u):
                    if not (isinstance(i, int) and i == 0):
                        dve.wait_ge(x1_stored[u], i * 16)
                    for t in range(TPB):
                        dve.wait_ge(proj_done, count(i, u, TPB, t + 1))
                        dve.tensor_tensor(x1[:, u, t], ps_p[:, t % 2], x_in[:, u, t], ALU.add).then_inc(resid_done, 1)
                        if t:
                            dve.wait_ge(resid_done, count(i, u, TPB, t))
                            dve.bn_stats(stats[:, t - 1], x1[:, u, t - 1]).then_inc(stats_done, 1)
                    dve.wait_ge(resid_done, count(i, u, TPB, TPB))
                    dve.bn_stats(stats[:, TPB - 1], x1[:, u, TPB - 1]).then_inc(stats_done, 1)
                    dve.wait_ge(stats_done, count(i, u, TPB, TPB))
                    dve.sem_inc(stats_seen, 1)
                    for t in range(TPB):
                        dve.bn_aggr(moments[:, t], stats[:, t]).then_inc(moments_done, 1)
                    dve.wait_ge(moments_done, count(i, u, TPB, TPB))
                    dve.tensor_scalar(var_eps[:], moments[:, :, 1], EPS, None, ALU.add).then_inc(eps_added, 1)

                def norm(i, u):
                    dve.wait_ge(rstd_done, count(i, u, 1, 1))
                    if not first(i, u):
                        dve.wait_ge(xt_in_psum, count(i, u, TPB, 0))
                    for t in range(TPB):
                        dve.tensor_scalar(x_norm[:, t], x1[:, u, t], moments[:, t, 0:1], rstd[:, t:t + 1],
                                          ALU.subtract, ALU.mult).then_inc(normed, 1)

                def transposed(i, u):
                    for t in range(TPB):
                        dve.wait_ge(xt_high, count(i, u, TPB, t + 1))
                        dve.tensor_tensor(xt_l[:, u, :, t * P:(t + 1) * P], ps_t[:, t % 2],
                                          xt_h[:, u, :, t * P:(t + 1) * P].bitcast(F32), ALU.subtract).then_inc(xt_low, 1)

                def group(i, u, g):
                    dve.wait_ge(group_high, count(i, u, DC, g + 1))
                    if g == 0 and not first(i, u):
                        dve.wait_ge(q_stored, count(i, u, 16 * Q_DMAS, 0))
                    dve.scalar_tensor_tensor(out=q_l[:, g], in0=ps_g[:, g], scalar=bq_sb[:, g:g + 1],
                                             in1=q_h[:, g].bitcast(F32), op0=ALU.add, op1=ALU.subtract)\
                       .then_inc(group_low, 1)

                def body(i, u, last):
                    i2, u2 = (i, 1) if u == 0 else (i + 1, 0)
                    if not last:
                        residual(i2, u2)
                        norm(i2, u2)
                    for g in range(DC):
                        group(i, u, g)
                    if not last:
                        transposed(i2, u2)
                        if not final_pair(i):
                            split(i + 1, u)

                split(0, 0)
                residual(0, 0)
                norm(0, 0)
                transposed(0, 0)
                split(0, 1)
                blocks(dve, body)

            @block.scalar
            def _(act):
                def split(i, u):
                    act.wait_ge(scaled, count(i, u, 1, 1))
                    if not first(i, u):
                        act.wait_ge(proj_done, count(i, u, TPB, 0))
                    act.activation(a_h[:], a_norm[:], ACT.Copy).then_inc(a_high, 1)

                def transposed(i, u):
                    for t in range(TPB):
                        act.wait_ge(xt_in_psum, count(i, u, TPB, t + 1))
                        act.activation(xt_h[:, u, :, t * P:(t + 1) * P], ps_t[:, t % 2], ACT.Copy).then_inc(xt_high, 1)

                def body(i, u, last):
                    for g in range(DC):
                        act.wait_ge(group_done, count(i, u, DC, g + 1))
                        if g == 0 and not first(i, u):
                            act.wait_ge(q_stored, count(i, u, 16 * Q_DMAS, 0))
                        act.activation(q_h[:, g], ps_g[:, g], ACT.Identity, bias=bq_sb[:, g:g + 1]).then_inc(group_high, 1)
                    if not last:
                        transposed(*((i, 1) if u == 0 else (i + 1, 0)))
                        if not final_pair(i):
                            split(i + 1, u)

                act.wait_ge(w_loaded, 64)
                split(0, 0)
                transposed(0, 0)
                split(0, 1)
                blocks(act, body)

            @block.tensor
            def _(pe):
                PARTS = ((0, 0), (0, 1), (1, 0))
                a, w, xt = (a_h, a_l), (w_h, w_l), (xt_h, xt_l)

                def project(i, u):
                    pe.wait_ge(a_low, count(i, u, 1, 1))
                    for t in range(TPB):
                        if not (first(i, u) and t < 2):
                            pe.wait_ge(resid_done, count(i, u, TPB, t - 1))
                        n = 0
                        for x, y in PARTS:
                            for c in range(DC):
                                mm = pe.matmul(ps_p[:, t % 2], a[x][:, c, t * P:(t + 1) * P], w[y][:, 0, c],
                                               start=(n == 0), stop=(n == 3 * DC - 1))
                                n += 1
                        mm.then_inc(proj_done, 1)

                def transposes(i, u):
                    for t in range(TPB):
                        pe.wait_ge(normed, count(i, u, TPB, t + 1))
                        if not (first(i, u) and t < 2):
                            pe.wait_ge(xt_low, count(i, u, TPB, t - 1))
                        for c in range(DC):
                            mm = pe.transpose(ps_t[:, t % 2, c], x_norm[:, t, c * P:(c + 1) * P], ident[:])
                        mm.then_inc(xt_in_psum, 1)

                def group(i, u, g):
                    if not first(i, u):
                        pe.wait_ge(group_low, count(i, u, DC, g + 1 - DC))
                    n = 0
                    for x, y in PARTS:
                        for c in range(DC):
                            mm = pe.matmul(ps_g[:, g], w[y][:, 1, c, g * P:(g + 1) * P], xt[x][:, u, c],
                                           start=(n == 0), stop=(n == 3 * DC - 1))
                            n += 1
                    mm.then_inc(group_done, 1)

                def body(i, u, last):
                    i2, u2 = (i, 1) if u == 0 else (i + 1, 0)
                    if not last:
                        project(i2, u2)
                    pe.wait_ge(xt_low, count(i, u, TPB, TPB))
                    for g in range(DC):
                        group(i, u, g)
                    if not last:
                        transposes(i2, u2)

                pe.wait_ge(w_low, 2)
                project(0, 0)
                transposes(0, 0)
                blocks(pe, body)


def cross_context(nc, ctx_t, wk_t, wv_t, bk_cols, bv, pad, pad_cols, causal_q, causal_k, xk_parts, xv_ones, mask_q, mask_k):
    with ExitStack() as ctx:
        sb = lambda name, shape, dt=F32: ctx.enter_context(nc.sbuf_tensor(name, shape, dt))
        sem = stage_semaphores(nc, ctx, "x_")
        ctx_sb = sb("ctx_sb", [P, DC, B * SC])
        wk_sb = sb("wk_sb", [P, DC, D])
        wv_sb = sb("wv_sb", [P, DC, D])
        bk_sb = sb("bk_sb", [P, DC])
        bv_sb = sb("bv_sb", [KH, D])
        kt = sb("kt", [P, B, DC, SC])
        kt_h = sb("kt_h", [P, B, DC, SC], F32R)
        kt_l = sb("kt_l", [P, B, DC, SC], F32R)
        xv = sb("xv", [KH, B, 2, H // 2, 3 * HD])
        pad_col = sb("pad_col", [KH, B, 2], U8)
        pad_row = sb("pad_row", [P, B, SC], U8)
        bias_col = sb("bias_col", [KH, B, 2])
        bias_row = sb("bias_row", [P, B, SC])
        cq = sb("cq", [P, TPB, SC])
        ck = sb("ck", [KH, 2, BLK])
        mq = sb("mq", [P, B, 2, TPB, SC], BF16)
        mk = sb("mk", [KH, B, 2, 2, BLK], BF16)
        ps = ctx.enter_context(nc.psum_tensor("ps_ctx", [P, 8, BLK], F32))
        loaded = {n: sem(f"{n}_loaded") for n in ("k", "v", "mask")}
        k_done, v_done, k_biased, k_high, k_low = (sem(n) for n in ("k_done", "v_done", "k_biased", "k_high", "k_low"))
        v_ready, ones_set, bias_done, masks_done, stored = (sem(n) for n in ("v_ready", "xv_ones_set", "bias_done", "masks_done", "ctx_stored"))

        with nc.Block() as block:

            @block.sync
            def _(sp):
                rows = lambda w: w.rearrange("(c p) n -> p c n", p=P)
                sp.dma_start(ctx_sb[:], rows(ctx_t)).then_inc(loaded["k"], 16)
                sp.dma_start(wk_sb[:], rows(wk_t)).then_inc(loaded["k"], 16)
                sp.dma_start(bk_sb[:], bk_cols).then_inc(loaded["k"], 16)
                sp.dma_start(wv_sb[:], rows(wv_t)).then_inc(loaded["v"], 16)
                sp.dma_start(bv_sb[:], bv.partition_broadcast(KH)).then_inc(loaded["v"], 16)
                sp.dma_start(pad_col[:], pad_cols).then_inc(loaded["mask"], 16)
                for b in range(B):
                    sp.dma_start(pad_row[:, b], pad[b].partition_broadcast(P)).then_inc(loaded["mask"], 16)
                sp.dma_start(cq[:], causal_q).then_inc(loaded["mask"], 16)
                sp.dma_start(ck[:], causal_k).then_inc(loaded["mask"], 16)
                sp.wait_ge(k_low, B)
                for g in range(P // HD):
                    for part, src in ((0, kt_h), (1, kt_h), (2, kt_l)):
                        dst = xk_parts[part * HD:(part + 1) * HD].rearrange("r b (c g) k -> g r (b c) k", g=P // HD)[g]
                        sp.dma_start(dst, src[g * HD:(g + 1) * HD].bitcast(F32).rearrange("r b c k -> r (b c) k"))\
                          .then_inc(stored, 16)
                sp.wait_ge(v_ready, 2 * B)
                sp.wait_ge(ones_set, 1)
                for b in range(B):
                    sp.dma_start(xv_ones[b], xv[:, b].rearrange("k h r c -> k (h r c)")).then_inc(stored, 16)
                sp.wait_ge(masks_done, 4 * B)
                sp.dma_start(mask_q, mq[:].rearrange("p b f t k -> p (b f t k)")).then_inc(stored, 16)
                sp.dma_start(mask_k, mk[:].rearrange("p b f h k -> p (b f h k)")).then_inc(stored, 16)
                sp.wait_ge(stored, 16 * (3 * (P // HD) + B + 2))

            @block.gpsimd
            def _(pool):
                pool.memset(xv[:, :, :, :, HD:2 * HD], 1.0).then_inc(ones_set, 1)

            @block.tensor
            def _(pe):
                pe.wait_ge(loaded["k"], 48)
                for c in range(DC):
                    for kc in range(DC):
                        mm = pe.matmul(ps[:, c, 0:B * SC], wk_sb[:, kc, c * P:(c + 1) * P], ctx_sb[:, kc],
                                       start=(kc == 0), stop=(kc == DC - 1))
                    mm.then_inc(k_done, 1)
                pe.wait_ge(loaded["v"], 32)
                for n in range(2 * B):
                    for kc in range(DC):
                        mm = pe.matmul(ps[0:KH, DC + n], ctx_sb[:, kc, n * KH:(n + 1) * KH], wv_sb[:, kc],
                                       start=(kc == 0), stop=(kc == DC - 1))
                    mm.then_inc(v_done, 1)

            @block.scalar
            def _(act):
                act.wait_ge(loaded["k"], 48)
                for c in range(DC):
                    act.wait_ge(k_done, c + 1)
                    act.activation(kt[:, :, c], ps[:, c, 0:B * SC].rearrange("p (b k) -> p b k", b=B), ACT.Identity,
                                   bias=bk_sb[:, c:c + 1]).then_inc(k_biased, 1)

            @block.vector
            def _(dve):
                dve.wait_ge(loaded["mask"], 16 * (B + 3))
                dve.tensor_scalar(bias_col[:], pad_col[:], MASKED, None, ALU.mult).then_inc(bias_done, 1)
                dve.tensor_scalar(bias_row[:], pad_row[:], MASKED, None, ALU.mult).then_inc(bias_done, 1)
                dve.wait_ge(bias_done, 2)
                for b in range(B):
                    for h in range(2):
                        col = bias_col[:, b, h:h + 1]
                        dve.tensor_scalar(mk[:, b, 0, h], ck[:, h], col, None, ALU.min)
                        mm = dve.tensor_scalar(mk[:, b, 1, h], ck[:, h], 0.0, col, ALU.mult, ALU.add)
                        mm.then_inc(masks_done, 1)
                    for t in range(TPB):
                        dve.tensor_tensor(mq[:, b, 0, t], cq[:, t], bias_row[:, b], ALU.min)
                        mm = dve.tensor_copy(mq[:, b, 1, t], bias_row[:, b])
                        if t % 2:
                            mm.then_inc(masks_done, 1)
                dve.wait_ge(k_biased, DC)
                for b in range(B):
                    dve.tensor_copy(kt_h[:, b], kt[:, b]).then_inc(k_high, 1)
                for b in range(B):
                    dve.wait_ge(k_high, b + 1)
                    dve.tensor_tensor(kt_l[:, b], kt[:, b], kt_h[:, b].bitcast(F32), ALU.subtract).then_inc(k_low, 1)
                for n in range(2 * B):
                    dve.wait_ge(v_done, n + 1)
                    dve.wait_ge(loaded["v"], 32)
                    dve.tensor_tensor(xv[:, n // 2, n % 2].rearrange("p r (a c) -> p r a c", c=HD)[:, :, 0::2],
                                      ps[0:KH, DC + n].rearrange("p (r a c) -> p r a c", a=2, c=HD),
                                      bv_sb[:].rearrange("p (r a c) -> p r a c", a=2, c=HD), ALU.add).then_inc(v_ready, 1)


def cross_attention(nc, q_parts, xk_parts, xv_ones, mask_q, mask_k, eye_bf, attn_t, sums):
    PAIRS = H // 2
    with ExitStack() as ctx:
        sb = lambda name, shape, dt=F32: ctx.enter_context(nc.sbuf_tensor(name, shape, dt))
        sem = stage_semaphores(nc, ctx, "d_")
        ROWS = 3 * HD
        TOP = ROWS + 3
        UPB = PAIRS
        BUFS = 4
        SCALE = float(HD) ** -0.5
        NM = 2 * TPB
        k_stack = sb("xk_stack", [TOP, BUFS, 2, SC], F32R)
        q_stack = sb("xq_stack", [TOP, BUFS, 2, BLK], F32R)
        v_ones = sb("xv_ones_sb", [KH, BUFS, 2, 3 * HD])
        mq = sb("mq_sb", [P, B, 2, TPB, SC], BF16)
        mk = sb("mk_sb", [KH, B, 2, 2, BLK], BF16)
        probs = sb("xprobs", [KH, 4, 2, BLK])
        neg_max = sb("xneg_max", [P, NM])
        rest = sb("xrest", [P, 2, NM])
        max_parts = sb("xmax_parts", [P, NM, 3], BF16)
        ident_bf = sb("xident_bf", [P, P], BF16)
        attn_out = sb("xattn_out", [P, 2, BLK])
        ps_st = ctx.enter_context(nc.psum_tensor("xps_st", [P, 2, BLK], F32))
        ps_s = ctx.enter_context(nc.psum_tensor("xps_s", [P, 2, 2, BLK], F32))
        ps_pv = ctx.enter_context(nc.psum_tensor("xps_pv", [P, 2, BLK], F32))

        loaded = [sem(f"xunit_loaded{s}") for s in range(BUFS)]
        consts_loaded, ones_set = sem("xconsts_loaded"), sem("xones_set")
        scores_done, max_done, chain = sem("xscores_done"), sem("xmax_done"), sem("xmax_chain")
        parts_done, max_turned, max_rows_done = sem("xparts_done"), sem("xmax_turned"), sem("xmax_rows_done")
        st_done, exp_done, pv_done, out_done = sem("xst_done"), sem("xexp_done"), sem("xpv_done"), sem("xout_done")
        out_stored = [sem(f"xout_stored{s}") for s in range(2)]
        ST_FREE, PV_FREE, PROBS_FREE = 2, 2, 2
        CHAIN, LOADS, OUT_DMAS = 4, 3, 3

        def at(i, w, per, c):
            return i * (UPB * per) + (w * per + c)

        def after(i, w, n):
            return (i + 1, w + n - UPB) if w + n >= UPB else (i, w + n)

        out_units = attn_t.rearrange("b (p j c) (n k) -> b p n j c k", p=PAIRS, j=2, n=BPB)
        sum_units = sums.rearrange("(u j) k -> u j k", j=2)

        with nc.Block() as block:

            @block.sync
            def _(sp):
                def load(n, w):
                    b = n // BPB
                    sp.dma_start(q_stack[0:ROWS, w % BUFS].bitcast(F32), q_parts[n, w]).then_inc(loaded[w % BUFS], 16)
                    sp.dma_start(k_stack[0:ROWS, w % BUFS].bitcast(F32), xk_parts[:, b, 2 * w:2 * w + 2]).then_inc(loaded[w % BUFS], 16)
                    sp.dma_start(v_ones[:, w % BUFS], xv_ones[b].rearrange("k (h r c) -> k h r c", h=2, r=PAIRS)[:, :, w])\
                      .then_inc(loaded[w % BUFS], 16)

                def body(i, last):
                    for w in range(UPB):
                        i2, w2 = after(i, w, BUFS)
                        if not last or w < UPB - BUFS + 2:
                            sp.wait_ge(pv_done, at(i, w, 1, 1))
                            load(i2 % NBLK, w2)
                        sp.wait_ge(out_done, at(i, w, 1, 1) + PV_FREE)
                        b, n = i // BPB, i % BPB
                        for j, row in ((0, 0), (1, 3 * HD)):
                            sp.dma_start(out_units[b, w, n, j], attn_out[row:row + HD, w % 2]).then_inc(out_stored[w % 2], 16)
                        sp.dma_start(sum_units[b * PAIRS + w].rearrange("j (n k) -> n j k", k=BLK)[n],
                                     attn_out[HD:3 * HD:HD, w % 2]).then_inc(out_stored[w % 2], 16)

                sp.dma_start(ident_bf[:], eye_bf).then_inc(consts_loaded, 16)
                sp.dma_start(mq[:].rearrange("p b f t k -> p (b f t k)"), mask_q).then_inc(consts_loaded, 16)
                sp.dma_start(mk[:].rearrange("p b f h k -> p (b f h k)"), mask_k).then_inc(consts_loaded, 16)
                for w in range(BUFS):
                    load(0, w)
                with sp.Fori(0, NBLK - 1) as i:
                    body(i, False)
                body(NBLK - 1, True)
                for s in range(2):
                    sp.wait_ge(out_stored[s], OUT_DMAS * 16 * NBLK * UPB // 2)

            @block.gpsimd
            def _(pool):
                pool.memset(k_stack[ROWS:TOP].bitcast(F32), 1.0).then_inc(ones_set, 1)

            @block.tensor
            def _(pe):
                def mask_of(mask, i):
                    n = i % NBLK if not isinstance(i, int) else i % NBLK
                    later = (n % BPB + (BPB - 1)) // BPB
                    return mask[:, n // BPB, later]

                def scores(i, w):
                    pe.wait_ge(loaded[w % BUFS], i * (LOADS * 16 * UPB // BUFS) + LOADS * 16 * (w // BUFS + 1))
                    for j in range(2):
                        if j == 0:
                            pe.wait_ge(max_done, at(i, w, 2, 0))
                        else:
                            pe.wait_ge(max_rows_done, at(i, w, 1, 0))
                        for t in range(TPB):
                            out = ps_s[:, (w + 1 + j) % 2, t // 2, (t % 2) * SC:(t % 2 + 1) * SC]
                            pe.matmul(out, q_stack[0:ROWS, w % BUFS, j, t * P:(t + 1) * P],
                                      k_stack[0:ROWS, w % BUFS, j], start=True, stop=False)
                            mm = pe.matmul(out, ident_bf[:], mask_of(mq, i)[:, t], start=False, stop=True)
                        mm.then_inc(scores_done, 1)

                def turn_max(i, w):
                    pe.wait_ge(parts_done, at(i, w, 1, 1))
                    for j in range(2):
                        for t in range(TPB):
                            mm = pe.matmul(ps_s[ROWS:TOP, (w + 1) % 2, j, t * P:(t + 1) * P],
                                           max_parts[:, j * TPB + t, :], ident_bf[:], start=True, stop=True)
                    mm.then_inc(max_turned, 1)

                def transposed_scores(i, w, j):
                    for h in range(2):
                        pe.wait_ge(exp_done, at(i, w, 4, 2 * j + h - 1) + ST_FREE)
                        pe.matmul(ps_st[0:KH, h], k_stack[:, w % BUFS, j, h * KH:(h + 1) * KH],
                                  q_stack[:, w % BUFS, j], start=True, stop=False)
                        pe.matmul(ps_st[0:KH, h], ident_bf[0:KH, 0:KH], mask_of(mk, i)[:, h],
                                  start=False, stop=True).then_inc(st_done, 1)

                def weighted_values(i, w):
                    pe.wait_ge(out_done, at(i, w, 1, 1))
                    pe.wait_ge(exp_done, at(i, w, 4, 4) + ST_FREE)
                    for h in range(2):
                        for j in range(2):
                            mm = pe.matmul(ps_pv[j * 2 * HD:(j + 1) * 2 * HD, w % 2],
                                           v_ones[:, w % BUFS, h, j * HD:(j + 2) * HD], probs[:, (w % 2) * 2 + j, h],
                                           start=(h == 0), stop=(h == 1))
                    mm.then_inc(pv_done, 1)

                pe.wait_ge(ones_set, 1)
                pe.wait_ge(consts_loaded, 48)
                scores(0, 0)
                turn_max(0, 0)
                scores(0, 1)
                with pe.Fori(0, NBLK) as i:
                    for w in range(UPB):
                        pe.wait_ge(max_rows_done, at(i, w, 1, 1))
                        transposed_scores(i, w, 0)
                        turn_max(*after(i, w, 1))
                        transposed_scores(i, w, 1)
                        scores(*after(i, w, 2))
                        weighted_values(i, w)

            @block.vector
            def _(dve):
                def maxima(i, w):
                    for j in range(2):
                        dve.wait_ge(scores_done, at(i, w, 2, j + 1))
                        dve.tensor_reduce(neg_max[:, j * TPB:(j + 1) * TPB],
                                          ps_s[:, (w + 1 + j) % 2, :, 0:2 * SC].rearrange("p a (t k) -> p a t k", k=SC),
                                          AX.X, ALU.max, negate=True).then_inc(max_done, 1)
                    dve.wait_ge(max_done, at(i, w, 2, 2))
                    left = neg_max[:]
                    for n in range(2):
                        if n:
                            dve.wait_ge(chain, at(i, w, CHAIN, 2 * n))
                        dve.tensor_copy(max_parts[:, :, n], left).then_inc(chain, 1)
                        dve.wait_ge(chain, at(i, w, CHAIN, 2 * n + 1))
                        dve.tensor_tensor(rest[:, n], left, max_parts[:, :, n], ALU.subtract).then_inc(chain, 1)
                        left = rest[:, n]
                    dve.wait_ge(chain, at(i, w, CHAIN, CHAIN))
                    dve.tensor_copy(max_parts[:, :, 2], left).then_inc(parts_done, 1)

                def max_rows(i, w):
                    dve.wait_ge(max_turned, at(i, w, 1, 1))
                    dve.tensor_copy(q_stack[ROWS:TOP, w % BUFS], ps_s[ROWS:TOP, (w + 1) % 2]).then_inc(max_rows_done, 1)

                maxima(0, 0)
                max_rows(0, 0)
                maxima(0, 1)
                with dve.Fori(0, NBLK) as i:
                    for w in range(UPB):
                        max_rows(*after(i, w, 1))
                        maxima(*after(i, w, 2))

            @block.scalar
            def _(act):
                act.sem_inc(exp_done, ST_FREE)
                act.sem_inc(out_done, PV_FREE)
                with act.Fori(0, NBLK) as i:
                    for w in range(UPB):
                        for j in range(2):
                            for h in range(2):
                                act.wait_ge(st_done, at(i, w, 4, 2 * j + h + 1))
                                act.activation(probs[:, (w % 2) * 2 + j, h], ps_st[0:KH, h], ACT.Exp, scale=SCALE).then_inc(exp_done, 1)
                        act.wait_ge(out_stored[w % 2], i * (OUT_DMAS * 16 * UPB // 2) + OUT_DMAS * 16 * (w // 2))
                        act.wait_ge(pv_done, at(i, w, 1, 1))
                        act.activation(attn_out[:, w % 2], ps_pv[:, w % 2], ACT.Copy).then_inc(out_done, 1)


def shared_feed_forward(nc, x1_rows, attn_t, sums, inv_sums, wo_t, bo, w12_t, b12, w3_t, b3, gamma, beta, eye,
                        h_rows, shared_rows, out_rows):
    with ExitStack() as ctx:
        sb = lambda name, shape, dt=F32: ctx.enter_context(nc.sbuf_tensor(name, shape, dt))
        sem = stage_semaphores(nc, ctx, "e_")
        w_h = sb("e_w_h", [P, 2, DC, D], F32R)
        w_l = sb("e_w_l", [P, 2, DC, D], F32R)
        w3_h = sb("e_w3_h", [P, HC, D], F32R)
        w3_l = sb("e_w3_l", [P, HC, D], F32R)
        bias_raw = sb("e_bias_raw", [1, 2 * D])
        bias_rows = sb("e_bias_rows", [P, 2 * D], F32R)
        ones_rows = sb("e_ones_rows", [P, P], F32R)
        bo_all = sb("bo_all", [P, D])
        gamma_all = sb("e_gamma_all", [P, HF])
        beta_all = sb("e_beta_all", [P, HF])
        ident = sb("e_identity", [P, P])
        sums_sb = sb("e_sums_sb", [P, BLK])
        inv_sb = sb("e_inv_sb", [P, BLK])
        a_raw = sb("e_a_raw", [P, 2, DC, BLK])
        a_inv = sb("e_a_inv", [P, DC, BLK])
        a_h = sb("e_a_h", [P, DC, BLK], F32R)
        a_l = sb("e_a_l", [P, DC, BLK], F32R)
        x_in = sb("e_x_in", [P, 2, TPB, D])
        x2 = sb("x2", [P, 2, TPB, D])
        h_out = sb("h_out", [P, 2, TPB, D])
        xt_h = sb("e_xt_h", [P, 2, DC, BLK], F32R)
        xt_l = sb("e_xt_l", [P, 2, DC, BLK], F32R)
        stats = sb("e_stats", [P, TPB, 6])
        moments = sb("e_moments", [P, TPB, 2])
        var_eps = sb("e_var_eps", [P, TPB])
        minus_half = sb("e_minus_half", [P, TPB])
        rstd = sb("e_rstd", [P, TPB])
        gated = sb("e_gated", [P, TPB, HF])
        z_stats = sb("e_z_stats", [P, TPB, 6])
        z_moments = sb("e_z_moments", [P, TPB, 2])
        z_var_eps = sb("e_z_var_eps", [P, TPB])
        z_rstd = sb("e_z_rstd", [P, TPB])
        zt_h = sb("e_zt_h", [P, TPB, HF], F32R)
        zt_l = sb("e_zt_l", [P, TPB, HF], F32R)
        shared_out = sb("shared_out", [P, TPB, D])
        out_sb = sb("out_sb", [P, TPB, D])
        wo_raw, w12_raw, w3_raw = h_out[:, 0], h_out[:, 1], shared_out[:, 0:HC]
        ps_t = ctx.enter_context(nc.psum_tensor("e_ps_t", [P, 2, DC, P], F32))
        ps_p = ctx.enter_context(nc.psum_tensor("e_ps_p", [P, 2, D], F32))
        ps_f = ctx.enter_context(nc.psum_tensor("e_ps_f", [P, 2, D], F32))
        ps_z = ctx.enter_context(nc.psum_tensor("e_ps_z", [P, 2, D], F32))

        w_loaded, w_high, w_low, consts = (sem(n) for n in ("w_loaded", "w_high", "w_low", "consts"))
        sums_loaded, inv_made, inv_stored = (sem(n) for n in ("sums_loaded", "inv_made", "inv_stored"))
        loaded = [sem(f"block_loaded{s}") for s in range(2)]
        LOADS = 2 + DC
        scaled, bo_added, a_high, a_low = (sem(n) for n in ("a_scaled", "bo_added", "a_high", "a_low"))
        proj_done, resid_done = sem("proj_done"), sem("resid_done")
        stats_done, moments_done, eps_added, rstd_done, normed, xt_in_psum, xt_high, xt_low = (
            sem(n) for n in ("stats_done", "moments_done", "eps_added", "rstd_done", "normed", "xt_in_psum",
                             "xt_high", "xt_low"))
        up_done, silu_done, gated_done, z_stats_done, z_moments_done, z_eps_added, z_rstd_done = (
            sem(n) for n in ("up_done", "silu_done", "gated_done", "z_stats_done", "z_moments_done", "z_eps_added",
                             "z_rstd_done"))
        z_normed, z_scaled, z_ready, zt_in_psum, zt_high, zt_low = (
            sem(n) for n in ("z_normed", "z_scaled", "z_ready", "zt_in_psum", "zt_high", "zt_low"))
        down_done, out_done, shared_done = (sem(n) for n in ("down_done", "out_done", "shared_done"))
        out_stored, shared_stored = sem("out_stored"), sem("shared_stored")
        h_stored = [sem(f"h_stored{s}") for s in range(2)]

        blocks_of = lambda rows: rows.rearrange("(n t p) d -> n p t d", t=TPB, p=P)
        x1_blocks, h_blocks, shared_blocks, out_blocks = (blocks_of(r) for r in (x1_rows, h_rows, shared_rows, out_rows))
        a_blocks = attn_t.rearrange("b (c p) (n k) -> b n p c k", p=P, k=BLK)
        inv_blocks = inv_sums.rearrange("(b c g) (n k) -> b n c g k", b=B, c=DC, k=BLK)

        def first(i, u):
            return isinstance(i, int) and i == 0 and u == 0

        def final_pair(i):
            return isinstance(i, int) and i == NBLK // 2 - 1

        def following(i, u):
            return (i, 1) if u == 0 else (i + 1, 0)

        def count(i, u, per, c):
            return i * (2 * per) + (u * per + c)

        def blocks(engine, body):
            body(0, 0, False)
            body(0, 1, False)
            with engine.Fori(1, NBLK // 2 - 1) as i:
                body(i, 0, False)
                body(i, 1, False)
            body(NBLK // 2 - 1, 0, False)
            body(NBLK // 2 - 1, 1, True)

        stats_seen = sem("stats_seen")
        z_stats_seen = sem("z_stats_seen")
        with nc.Block() as block:

            @block.sync
            def _(sp):
                def load(n, i, u):
                    b, k = n // BPB, n % BPB
                    sp.dma_start(a_raw[:, u], a_blocks[b, k]).then_inc(loaded[u], 16)
                    sp.dma_start(x_in[:, u], x1_blocks[n]).then_inc(loaded[u], 16)
                    if not first(i, u):
                        sp.wait_ge(scaled, count(i, u, 1, 0))
                    for c in range(DC):
                        src = inv_blocks[b, k, c].unsqueeze(1).to_broadcast([P // HD, HD, BLK])
                        sp.dma_start(a_inv[:, c], src).then_inc(loaded[u], 16)

                sp.dma_start(sums_sb[:], sums.rearrange("h (n k) -> (h n) k", k=BLK)).then_inc(sums_loaded, 16)
                rows = lambda w: w.rearrange("(c p) n -> p c n", p=P)
                for dst, src in ((ident[:], eye), (wo_raw, rows(wo_t)), (w12_raw, rows(w12_t)), (w3_raw, rows(w3_t)),
                                 (bias_raw[:, 0:D], b12.unsqueeze(0)), (bias_raw[:, D:2 * D], b3.unsqueeze(0)),
                                 (bo_all[:], bo.partition_broadcast(P)), (gamma_all[:], gamma.partition_broadcast(P)),
                                 (beta_all[:], beta.partition_broadcast(P))):
                    sp.dma_start(dst, src).then_inc(w_loaded, 16)
                sp.wait_ge(inv_made, 1)
                sp.dma_start(inv_sums.rearrange("h (n k) -> (h n) k", k=BLK), inv_sb[:]).then_inc(inv_stored, 16)
                sp.wait_ge(inv_stored, 16)
                load(0, 0, 0)
                load(1, 0, 1)

                def advance(i, u, more):
                    if more:
                        sp.wait_ge(resid_done, count(i, u, TPB, TPB))
                        load(2 * i + (u + 2), i + 1, u)
                    sp.wait_ge(normed, count(i, u, TPB, TPB))
                    sp.dma_start(h_blocks[2 * i + u], h_out[:, u]).then_inc(h_stored[u], 16)

                def body(i, u, last):
                    if not last:
                        i2, u2 = following(i, u)
                        advance(i2, u2, not (final_pair(i) or (isinstance(i, int) and i == NBLK // 2 - 2 and u == 1)))
                    sp.wait_ge(shared_done, count(i, u, TPB, TPB))
                    sp.dma_start(shared_blocks[2 * i + u], shared_out[:]).then_inc(shared_stored, 16)
                    sp.wait_ge(out_done, count(i, u, TPB, TPB))
                    sp.dma_start(out_blocks[2 * i + u], out_sb[:]).then_inc(out_stored, 16)

                advance(0, 0, True)
                body(0, 0, False)
                body(0, 1, False)
                with sp.Fori(1, NBLK // 2 - 2) as i:
                    body(i, 0, False)
                    body(i, 1, False)
                for i in range(NBLK // 2 - 2, NBLK // 2):
                    body(i, 0, False)
                    body(i, 1, i == NBLK // 2 - 1)
                for s in range(2):
                    sp.wait_ge(h_stored[s], 16 * NBLK // 2)
                sp.wait_ge(shared_stored, 16 * NBLK)
                sp.wait_ge(out_stored, 16 * NBLK)

            @block.gpsimd
            def _(pool):
                def scale(i, u):
                    pool.wait_ge(loaded[u], i * (16 * LOADS) + 16 * LOADS)
                    pool.tensor_tensor(a_raw[:, u], a_raw[:, u], a_inv[:], ALU.mult).then_inc(scaled, 1)
                    for t in range(TPB):
                        pool.tensor_tensor(x_in[:, u, t], x_in[:, u, t], bo_all[:], ALU.add).then_inc(bo_added, 1)

                def z_affine(i, u):
                    pool.wait_ge(z_eps_added, count(i, u, 1, 1))
                    pool.tensor_tensor(z_rstd[:], z_var_eps[:], minus_half[:], ALU.pow).then_inc(z_rstd_done, 1)
                    for t in range(TPB):
                        pool.wait_ge(z_normed, count(i, u, TPB, t + 1))
                        pool.tensor_tensor(gated[:, t], gated[:, t], gamma_all[:], ALU.mult).then_inc(z_scaled, 1)
                        pool.wait_ge(z_scaled, count(i, u, TPB, t + 1))
                        pool.tensor_tensor(gated[:, t], gated[:, t], beta_all[:], ALU.add).then_inc(z_ready, 1)

                def rsqrt(i, u):
                    pool.wait_ge(eps_added, count(i, u, 1, 1))
                    pool.tensor_tensor(rstd[:], var_eps[:], minus_half[:], ALU.pow).then_inc(rstd_done, 1)

                def body(i, u, last):
                    z_affine(i, u)
                    if not last:
                        rsqrt(*following(i, u))
                        if not final_pair(i):
                            scale(i + 1, u)

                pool.memset(bias_rows[:].bitcast(F32), 0.0).then_inc(consts, 1)
                pool.memset(ones_rows[:].bitcast(F32), 0.0).then_inc(consts, 1)
                pool.memset(minus_half[:], -0.5).then_inc(consts, 1)
                pool.wait_ge(consts, 3)
                for row in (0, 32):
                    pool.memset(ones_rows[row:row + 1].bitcast(F32), 1.0).then_inc(consts, 1)
                pool.wait_ge(consts, 5)
                pool.wait_ge(w_loaded, 9 * 16)
                scale(0, 0)
                scale(0, 1)
                rsqrt(0, 0)
                blocks(pool, body)

            @block.vector
            def _(dve):
                dve.wait_ge(sums_loaded, 16)
                dve.reciprocal(inv_sb[:], sums_sb[:]).then_inc(inv_made, 1)
                dve.wait_ge(w_loaded, 9 * 16)
                dve.wait_ge(consts, 3)
                splits = ((wo_raw, w_h[:, 0], w_l[:, 0]), (w12_raw, w_h[:, 1], w_l[:, 1]), (w3_raw, w3_h[:], w3_l[:]),
                          (bias_raw[:], bias_rows[0:1], bias_rows[32:33]))
                for raw, high, _ in splits:
                    dve.tensor_copy(high, raw).then_inc(w_high, 1)
                for n, (raw, high, low) in enumerate(splits):
                    dve.wait_ge(w_high, n + 1)
                    dve.tensor_tensor(low, raw, high.bitcast(F32), ALU.subtract).then_inc(w_low, 1)

                def split(i, u):
                    dve.wait_ge(a_high, count(i, u, 1, 1))
                    if not first(i, u):
                        dve.wait_ge(proj_done, count(i, u, TPB, 0))
                    dve.tensor_tensor(a_l[:], a_raw[:, u], a_h[:].bitcast(F32), ALU.subtract).then_inc(a_low, 1)

                def residual(i, u):
                    dve.wait_ge(bo_added, count(i, u, TPB, TPB))
                    for t in range(TPB):
                        dve.wait_ge(proj_done, count(i, u, TPB, t + 1))
                        dve.tensor_tensor(x2[:, u, t], ps_p[:, t % 2], x_in[:, u, t], ALU.add).then_inc(resid_done, 1)
                        if t:
                            dve.wait_ge(resid_done, count(i, u, TPB, t))
                            dve.bn_stats(stats[:, t - 1], x2[:, u, t - 1]).then_inc(stats_done, 1)
                    dve.wait_ge(resid_done, count(i, u, TPB, TPB))
                    dve.bn_stats(stats[:, TPB - 1], x2[:, u, TPB - 1]).then_inc(stats_done, 1)
                    dve.wait_ge(stats_done, count(i, u, TPB, TPB))
                    dve.sem_inc(stats_seen, 1)
                    for t in range(TPB):
                        dve.bn_aggr(moments[:, t], stats[:, t]).then_inc(moments_done, 1)
                    dve.wait_ge(moments_done, count(i, u, TPB, TPB))
                    dve.tensor_scalar(var_eps[:], moments[:, :, 1], EPS, None, ALU.add).then_inc(eps_added, 1)

                def norm(i, u):
                    dve.wait_ge(rstd_done, count(i, u, 1, 1))
                    if not first(i, u):
                        dve.wait_ge(xt_in_psum, count(i, u, TPB, 0))
                    if not (isinstance(i, int) and i == 0):
                        dve.wait_ge(h_stored[u], i * 16)
                    for t in range(TPB):
                        dve.tensor_scalar(h_out[:, u, t], x2[:, u, t], moments[:, t, 0:1], rstd[:, t:t + 1],
                                          ALU.subtract, ALU.mult).then_inc(normed, 1)

                def transposed(i, u):
                    for t in range(TPB):
                        dve.wait_ge(xt_high, count(i, u, TPB, t + 1))
                        dve.tensor_tensor(xt_l[:, u, :, t * P:(t + 1) * P], ps_t[:, t % 2],
                                          xt_h[:, u, :, t * P:(t + 1) * P].bitcast(F32), ALU.subtract).then_inc(xt_low, 1)

                def gate(i, u):
                    for t in range(TPB):
                        dve.wait_ge(silu_done, count(i, u, TPB, t + 1))
                        dve.tensor_tensor(gated[:, t], ps_f[:, t % 2, HF:D], gated[:, t], ALU.mult).then_inc(gated_done, 1)
                        if t:
                            dve.wait_ge(gated_done, count(i, u, TPB, t))
                            dve.bn_stats(z_stats[:, t - 1], gated[:, t - 1]).then_inc(z_stats_done, 1)
                    dve.wait_ge(gated_done, count(i, u, TPB, TPB))
                    dve.bn_stats(z_stats[:, TPB - 1], gated[:, TPB - 1]).then_inc(z_stats_done, 1)
                    dve.wait_ge(z_stats_done, count(i, u, TPB, TPB))
                    dve.sem_inc(z_stats_seen, 1)
                    for t in range(TPB):
                        dve.bn_aggr(z_moments[:, t], z_stats[:, t]).then_inc(z_moments_done, 1)
                    dve.wait_ge(z_moments_done, count(i, u, TPB, TPB))
                    dve.tensor_scalar(z_var_eps[:], z_moments[:, :, 1], EPS, None, ALU.add).then_inc(z_eps_added, 1)
                    dve.wait_ge(z_rstd_done, count(i, u, 1, 1))
                    for t in range(TPB):
                        dve.tensor_scalar(gated[:, t], gated[:, t], z_moments[:, t, 0:1], z_rstd[:, t:t + 1],
                                          ALU.subtract, ALU.mult).then_inc(z_normed, 1)

                def z_split(i, u, t):
                    dve.wait_ge(zt_high, count(i, u, TPB, t + 1))
                    dve.tensor_tensor(zt_l[:, t], ps_z[:, t % 2, 0:HF], zt_h[:, t].bitcast(F32), ALU.subtract)\
                       .then_inc(zt_low, 1)

                def output(i, u, t):
                    dve.wait_ge(shared_done, count(i, u, TPB, t + 1))
                    if t == 0 and not first(i, u):
                        dve.wait_ge(out_stored, count(i, u, 16, 0))
                    dve.tensor_tensor(out_sb[:, t], ps_f[:, t % 2], x2[:, u, t], ALU.add).then_inc(out_done, 1)

                def body(i, u, last):
                    gate(i, u)
                    if not last:
                        residual(*following(i, u))
                        norm(*following(i, u))
                    for t in range(TPB + 1):
                        if t < TPB:
                            z_split(i, u, t)
                        if t:
                            output(i, u, t - 1)
                    if not last:
                        transposed(*following(i, u))
                        if not final_pair(i):
                            split(i + 1, u)

                split(0, 0)
                residual(0, 0)
                norm(0, 0)
                transposed(0, 0)
                split(0, 1)
                blocks(dve, body)

            @block.scalar
            def _(act):
                def split(i, u):
                    act.wait_ge(scaled, count(i, u, 1, 1))
                    if not first(i, u):
                        act.wait_ge(proj_done, count(i, u, TPB, 0))
                    act.activation(a_h[:], a_raw[:, u], ACT.Copy).then_inc(a_high, 1)

                def transposed(i, u):
                    for t in range(TPB):
                        act.wait_ge(xt_in_psum, count(i, u, TPB, t + 1))
                        act.activation(xt_h[:, u, :, t * P:(t + 1) * P], ps_t[:, t % 2], ACT.Copy).then_inc(xt_high, 1)

                def body(i, u, last):
                    for t in range(TPB):
                        act.wait_ge(up_done, count(i, u, TPB, t + 1))
                        act.activation(gated[:, t], ps_f[:, t % 2, 0:HF], ACT.Silu).then_inc(silu_done, 1)
                    for t in range(TPB + 1):
                        if t < TPB:
                            act.wait_ge(zt_in_psum, count(i, u, TPB, t + 1))
                            act.activation(zt_h[:, t], ps_z[:, t % 2, 0:HF], ACT.Copy).then_inc(zt_high, 1)
                        if t:
                            if t == 1 and not first(i, u):
                                act.wait_ge(shared_stored, count(i, u, 16, 0))
                            act.wait_ge(down_done, count(i, u, TPB, t))
                            act.activation(shared_out[:, t - 1], ps_f[:, (t - 1) % 2], ACT.Copy).then_inc(shared_done, 1)
                    if not last:
                        transposed(*following(i, u))
                        if not final_pair(i):
                            split(i + 1, u)

                split(0, 0)
                transposed(0, 0)
                split(0, 1)
                act.wait_ge(w_low, 3)
                blocks(act, body)

            @block.tensor
            def _(pe):
                PARTS = ((0, 0), (0, 1), (1, 0))
                a, w, w3, xt, zt = (a_h, a_l), (w_h, w_l), (w3_h, w3_l), (xt_h, xt_l), (zt_h, zt_l)

                def project(i, u):
                    pe.wait_ge(a_low, count(i, u, 1, 1))
                    for t in range(TPB):
                        if not (first(i, u) and t < 2):
                            pe.wait_ge(resid_done, count(i, u, TPB, t - 1))
                        n = 0
                        for x, y in PARTS:
                            for c in range(DC):
                                mm = pe.matmul(ps_p[:, t % 2], a[x][:, c, t * P:(t + 1) * P], w[y][:, 0, c],
                                               start=(n == 0), stop=(n == 3 * DC - 1))
                                n += 1
                        mm.then_inc(proj_done, 1)

                def transposes(i, u):
                    for t in range(TPB):
                        pe.wait_ge(normed, count(i, u, TPB, t + 1))
                        if not (first(i, u) and t < 2):
                            pe.wait_ge(xt_low, count(i, u, TPB, t - 1))
                        for c in range(DC):
                            mm = pe.transpose(ps_t[:, t % 2, c], h_out[:, u, t, c * P:(c + 1) * P], ident[:])
                        mm.then_inc(xt_in_psum, 1)

                def up(i, u, t):
                    if t >= 2:
                        pe.wait_ge(gated_done, count(i, u, TPB, t - 1))
                    elif not first(i, u):
                        pe.wait_ge(out_done, count(i, u, TPB, t - 1))
                    pe.matmul(ps_f[:, t % 2], ones_rows[:], bias_rows[:, 0:D], start=True, stop=False)
                    n = 0
                    for x, y in PARTS:
                        for c in range(DC):
                            mm = pe.matmul(ps_f[:, t % 2], xt[x][:, u, c, t * P:(t + 1) * P], w[y][:, 1, c],
                                           start=False, stop=(n == 3 * DC - 1))
                            n += 1
                    mm.then_inc(up_done, 1)

                def z_transposes(i, u, t):
                    pe.wait_ge(z_ready, count(i, u, TPB, t + 1))
                    if not (first(i, u) and t < 2):
                        pe.wait_ge(zt_low, count(i, u, TPB, t - 1))
                    for c in range(HC):
                        mm = pe.transpose(ps_z[:, t % 2, c * P:(c + 1) * P], gated[:, t, c * P:(c + 1) * P], ident[:])
                    mm.then_inc(zt_in_psum, 1)

                def down(i, u, t):
                    if t < 2:
                        pe.wait_ge(gated_done, count(i, u, TPB, t + 3))
                    else:
                        pe.wait_ge(out_done, count(i, u, TPB, t - 1))
                    pe.wait_ge(zt_low, count(i, u, TPB, t + 1))
                    pe.matmul(ps_f[:, t % 2], ones_rows[:], bias_rows[:, D:2 * D], start=True, stop=False)
                    n = 0
                    for x, y in PARTS:
                        for c in range(HC):
                            mm = pe.matmul(ps_f[:, t % 2], zt[x][:, t, c * P:(c + 1) * P], w3[y][:, c],
                                           start=False, stop=(n == 3 * HC - 1))
                            n += 1
                    mm.then_inc(down_done, 1)

                def body(i, u, last):
                    pe.wait_ge(xt_low, count(i, u, TPB, TPB))
                    for t in range(TPB):
                        up(i, u, t)
                    if not last:
                        project(*following(i, u))
                    for t in range(TPB + 1):
                        if t < TPB:
                            z_transposes(i, u, t)
                        if t:
                            down(i, u, t - 1)
                    if not last:
                        transposes(*following(i, u))

                pe.wait_ge(w_low, 4)
                pe.wait_ge(consts, 5)
                project(0, 0)
                transposes(0, 0)
                blocks(pe, body)


def selected_experts(nc, h_rows, shared_rows, out_rows, index_b, index_t, gate_t, gate_bias, exp_bias,
                     w12_t, w3_t, bias, gamma, beta, eye):
    MT = M // P
    G = E + 1
    GP = G + G % 2
    RING = 4
    LAG_Z, LAG_DOWN, LAG_ACC = 2, 3, 4
    with ExitStack() as ctx:
        sb = lambda name, shape, dt=F32: ctx.enter_context(nc.sbuf_tensor(name, shape, dt))
        sem = stage_semaphores(nc, ctx, "f_")
        idx_b, idx_t = sb("idx_b", [P, MT], I32), sb("idx_t", [P, MT], I32)
        wrap_b, wrap_t = sb("wrap_b", [P, MT], I32), sb("wrap_t", [P, MT], I32)
        row_b, row_idx = sb("row_b", [P, MT], I32), sb("row_idx", [P, MT], I32)
        acc = sb("acc", [P, MT, D])
        h_sel = sb("h_sel", [P, MT, D])
        shared_sel = sb("shared_sel", [P, MT, D])
        ht_h, ht_l = sb("ht_h", [P, DC, M], F32R), sb("ht_l", [P, DC, M], F32R)
        gate_raw = sb("gate_raw", [P, DC, GP])
        gate_h, gate_l = sb("gate_h", [P, DC, GP], F32R), sb("gate_l", [P, DC, GP], F32R)
        gate_bias_all, exp_bias_all = sb("gate_bias_all", [P, G]), sb("exp_bias_all", [P, E])
        logits, scores = sb("logits", [P, MT, G]), sb("scores", [P, MT, G])
        biased, at_max = sb("biased", [P, MT, E]), sb("at_max", [P, MT, E])
        order = sb("order", [P, E])
        best, first_best = sb("best", [P, MT]), sb("first_best", [P, MT])
        one_hot, picked = sb("one_hot", [P, MT, E]), sb("picked", [P, MT, E])
        top_score, share, neg_share = sb("top_score", [P, MT]), sb("share", [P, MT]), sb("neg_share", [P, MT])
        coefs = sb("coefs", [P, E, MT])
        coef = sb("coef", [P, 2, MT])
        w12_raw, w3_raw = sb("f_w12_raw", [P, 2, DC, D]), sb("f_w3_raw", [P, 2, HC, D])
        w12_h, w12_l = sb("f_w12_h", [P, 2, DC, D], F32R), sb("f_w12_l", [P, 2, DC, D], F32R)
        w3_h, w3_l = sb("f_w3_h", [P, 2, HC, D], F32R), sb("f_w3_l", [P, 2, HC, D], F32R)
        bias_raw = sb("f_bias_raw", [1, 2, 2 * D])
        bias_rows = sb("f_bias_rows", [P, 2, 2 * D], F32R)
        ones_rows = sb("f_ones_rows", [P, P], F32R)
        gamma_all, beta_all = sb("f_gamma_all", [P, HF]), sb("f_beta_all", [P, HF])
        ident = sb("f_identity", [P, P])
        gated = sb("f_gated", [P, RING, HF])
        z_stats, z_moments = sb("f_z_stats", [P, 2, 6]), sb("f_z_moments", [P, 2, 2])
        z_var_eps, z_rstd, minus_half = sb("f_z_var_eps", [P, 2]), sb("f_z_rstd", [P, 2]), sb("f_minus_half", [P, 1])
        zt_h, zt_l = sb("f_zt_h", [P, 2, HF], F32R), sb("f_zt_l", [P, 2, HF], F32R)
        ps_t = ctx.enter_context(nc.psum_tensor("f_ps_t", [P, 2, DC, P], F32))
        ps_u = ctx.enter_context(nc.psum_tensor("f_ps_u", [P, 2, D], F32))
        ps_d = ctx.enter_context(nc.psum_tensor("f_ps_d", [P, 2, D], F32))
        ps_z = ctx.enter_context(nc.psum_tensor("f_ps_z", [P, 2, D], F32))

        idx_loaded, consts, small_loaded = sem("idx_loaded"), sem("consts"), sem("small_loaded")
        idx_done, h_gathered, shared_gathered, out_gathered = (
            sem(n) for n in ("idx_done", "h_gathered", "shared_gathered", "out_gathered"))
        ht_in_psum, ht_high, ht_low, gate_split = (sem(n) for n in ("ht_in_psum", "ht_high", "ht_low", "gate_split"))
        logits_in_psum, biased_logits, scored, routed, exped = (
            sem(n) for n in ("logits_in_psum", "biased_logits", "scored", "routed", "exped"))
        loaded = [sem(f"weights_loaded{s}") for s in range(2)]
        w12_high, w3_high, w12_low, w3_low, bias_high, bias_low = (
            sem(n) for n in ("w12_high", "w3_high", "w12_low", "w3_low", "bias_high", "bias_low"))
        up_done, silu_done, gated_done, stats_done, moments_done, eps_added, rstd_done, normed = (
            sem(n) for n in ("up_done", "silu_done", "gated_done", "stats_done", "moments_done", "eps_added",
                             "rstd_done", "normed"))
        scaled, z_ready, zt_in_psum, zt_high, zt_low, down_done, acc_done, coef_set = (
            sem(n) for n in ("scaled", "z_ready", "zt_in_psum", "zt_high", "zt_low", "down_done", "acc_done",
                             "coef_set"))
        scattered = sem("scattered")
        SMALL = 6
        LOADS = 3
        PAIR = 2 * MT

        def steps(engine, step):
            for s in range(LAG_ACC):
                step(0, s)
            with engine.Fori(0, E // 2 - 1) as i:
                for s in range(LAG_ACC, PAIR + LAG_ACC):
                    step(i, s)
            for s in range(LAG_ACC, PAIR + LAG_ACC):
                step(E // 2 - 1, s)

        def draining(i, s):
            return isinstance(i, int) and i == E // 2 - 1 and s >= PAIR

        def splits_next(i, s, at):
            return s % MT == at and not (isinstance(i, int) and i == E // 2 - 1 and s >= MT)

        stats_seen = sem("stats_seen")
        with nc.Block() as block:

            @block.sync
            def _(sp):
                def load(e, s):
                    sp.dma_start(w12_raw[:, s], w12_t[e].rearrange("(c p) n -> p c n", p=P)).then_inc(loaded[s], 16)
                    sp.dma_start(w3_raw[:, s], w3_t[e].rearrange("(c p) n -> p c n", p=P)).then_inc(loaded[s], 16)
                    sp.dma_start(bias_raw[:, s], bias[e].unsqueeze(0)).then_inc(loaded[s], 16)

                sp.dma_start(idx_b[:], index_b).then_inc(idx_loaded, 16)
                sp.dma_start(idx_t[:], index_t).then_inc(idx_loaded, 16)
                sp.dma_start(ident[:], eye).then_inc(small_loaded, 16)
                sp.wait_ge(consts, 4)
                sp.dma_start(gate_raw[:, :, 0:G], gate_t.rearrange("(c p) n -> p c n", p=P)).then_inc(small_loaded, 16)
                sp.dma_start(gate_bias_all[:], gate_bias.partition_broadcast(P)).then_inc(small_loaded, 16)
                sp.dma_start(exp_bias_all[:], exp_bias.partition_broadcast(P)).then_inc(small_loaded, 16)
                sp.dma_start(gamma_all[:], gamma.partition_broadcast(P)).then_inc(small_loaded, 16)
                sp.dma_start(beta_all[:], beta.partition_broadcast(P)).then_inc(small_loaded, 16)
                load(0, 0)
                load(1, 1)
                with sp.Fori(1, E // 2) as i:
                    for s in range(2):
                        sp.wait_ge(w12_low, i * 2 + (s - 1))
                        sp.wait_ge(w3_low, i * 2 + (s - 1))
                        sp.wait_ge(bias_low, i * 2 + (s - 1))
                        load(i * 2 + s, s)

            @block.gpsimd
            def _(pool):
                pool.memset(bias_rows[:].bitcast(F32), 0.0).then_inc(consts, 1)
                pool.memset(ones_rows[:].bitcast(F32), 0.0).then_inc(consts, 1)
                pool.memset(minus_half[:], -0.5).then_inc(consts, 1)
                pool.memset(gate_raw[:], 0.0).then_inc(consts, 1)
                pool.wait_ge(consts, 4)
                for row in (0, 32):
                    pool.memset(ones_rows[row:row + 1].bitcast(F32), 1.0).then_inc(consts, 1)
                pool.wait_ge(consts, 6)
                for e in range(E):
                    pool.memset(order[:, e:e + 1], float(E - e)).then_inc(consts, 1)
                pool.wait_ge(idx_done, 5)
                for rows, target, done in ((h_rows, h_sel, h_gathered), (shared_rows, shared_sel, shared_gathered),
                                           (out_rows, acc, out_gathered)):
                    for m in range(MT):
                        pool.indirect_dma_start(target[:, m], None, rows,
                                                bass.IndirectOffsetOnAxis(row_idx[:, m:m + 1], axis=0)).then_inc(done, 16)
                pool.wait_ge(consts, 6 + E)
                pool.wait_ge(small_loaded, 16 * SMALL)

                def step(i, s):
                    if draining(i, s):
                        return
                    pool.wait_ge(eps_added, i * PAIR + (s + 1))
                    pool.tensor_tensor(z_rstd[:, s % 2:s % 2 + 1], z_var_eps[:, s % 2:s % 2 + 1], minus_half[:], ALU.pow)\
                        .then_inc(rstd_done, 1)
                    pool.wait_ge(normed, i * PAIR + (s + 1))
                    pool.tensor_tensor(gated[:, s % RING], gated[:, s % RING], gamma_all[:], ALU.mult).then_inc(scaled, 1)
                    pool.wait_ge(scaled, i * PAIR + (s + 1))
                    pool.tensor_tensor(gated[:, s % RING], gated[:, s % RING], beta_all[:], ALU.add).then_inc(z_ready, 1)

                steps(pool, step)
                pool.wait_ge(out_gathered, 16 * MT)
                for m in range(MT):
                    pool.wait_ge(acc_done, MT + (E - 1) * MT + m + 1)
                    pool.indirect_dma_start(out_rows, bass.IndirectOffsetOnAxis(row_idx[:, m:m + 1], axis=0),
                                            acc[:, m], None).then_inc(scattered, 16)
                pool.wait_ge(scattered, 16 * MT)

            @block.vector
            def _(dve):
                dve.wait_ge(idx_loaded, 2 * 16)
                dve.tensor_scalar(wrap_b[:], idx_b[:], 0, B, ALU.is_lt, ALU.mult).then_inc(idx_done, 1)
                dve.tensor_scalar(wrap_t[:], idx_t[:], 0, S, ALU.is_lt, ALU.mult).then_inc(idx_done, 1)
                dve.wait_ge(idx_done, 2)
                dve.tensor_tensor(row_b[:], idx_b[:], wrap_b[:], ALU.add).then_inc(idx_done, 1)
                dve.tensor_tensor(wrap_t[:], idx_t[:], wrap_t[:], ALU.add).then_inc(idx_done, 1)
                dve.wait_ge(idx_done, 4)
                dve.scalar_tensor_tensor(out=row_idx[:], in0=row_b[:], scalar=float(S), in1=wrap_t[:], op0=ALU.mult,
                                         op1=ALU.add).then_inc(idx_done, 1)
                dve.wait_ge(small_loaded, 16 * SMALL)
                dve.tensor_copy(gate_h[:], gate_raw[:]).then_inc(gate_split, 1)
                dve.wait_ge(gate_split, 1)
                dve.tensor_tensor(gate_l[:], gate_raw[:], gate_h[:].bitcast(F32), ALU.subtract).then_inc(gate_split, 1)

                def split_w12(n, s):
                    dve.wait_ge(w12_high, n + 1)
                    dve.tensor_tensor(w12_l[:, s], w12_raw[:, s], w12_h[:, s].bitcast(F32), ALU.subtract).then_inc(w12_low, 1)

                def split_w3(n, s):
                    dve.wait_ge(w3_high, n + 1)
                    dve.tensor_tensor(w3_l[:, s], w3_raw[:, s], w3_h[:, s].bitcast(F32), ALU.subtract).then_inc(w3_low, 1)

                def split_bias(n, s):
                    dve.wait_ge(w3_high, n + 1)
                    dve.tensor_copy(bias_rows[0:1, s], bias_raw[:, s]).then_inc(bias_high, 1)
                    dve.wait_ge(bias_high, n + 1)
                    dve.tensor_tensor(bias_rows[32:33, s], bias_raw[:, s], bias_rows[0:1, s].bitcast(F32), ALU.subtract)\
                       .then_inc(bias_low, 1)

                dve.wait_ge(consts, 2)
                split_w12(0, 0)
                split_w3(0, 0)
                split_bias(0, 0)
                for m in range(MT):
                    dve.wait_ge(ht_high, m + 1)
                    cols = slice(m * P, (m + 1) * P)
                    dve.tensor_tensor(ht_l[:, :, cols], ps_t[:, m % 2], ht_h[:, :, cols].bitcast(F32), ALU.subtract)\
                       .then_inc(ht_low, 1)
                    if m:
                        dve.wait_ge(logits_in_psum, m)
                        dve.tensor_tensor(logits[:, m - 1], ps_z[:, (m - 1) % 2, 0:G], gate_bias_all[:], ALU.add)\
                           .then_inc(biased_logits, 1)
                dve.wait_ge(logits_in_psum, MT)
                dve.tensor_tensor(logits[:, MT - 1], ps_z[:, (MT - 1) % 2, 0:G], gate_bias_all[:], ALU.add)\
                   .then_inc(biased_logits, 1)

                def over_tiles(row):
                    return row.unsqueeze(1).to_broadcast([P, MT, E])

                def over_experts(column):
                    return column.unsqueeze(2).to_broadcast([P, MT, E])

                dve.wait_ge(scored, 1)
                dve.wait_ge(consts, 6 + E)
                dve.tensor_tensor(biased[:], scores[:, :, 1:G], over_tiles(exp_bias_all[:]), ALU.add).then_inc(routed, 1)
                dve.wait_ge(routed, 1)
                dve.tensor_reduce(best[:], biased[:], AX.X, ALU.max).then_inc(routed, 1)
                dve.wait_ge(routed, 2)
                dve.tensor_tensor(at_max[:], biased[:], over_experts(best[:]), ALU.is_ge).then_inc(routed, 1)
                dve.wait_ge(routed, 3)
                dve.tensor_tensor(at_max[:], at_max[:], over_tiles(order[:]), ALU.mult).then_inc(routed, 1)
                dve.wait_ge(routed, 4)
                dve.tensor_reduce(first_best[:], at_max[:], AX.X, ALU.max).then_inc(routed, 1)
                dve.wait_ge(routed, 5)
                dve.tensor_tensor(one_hot[:], at_max[:], over_experts(first_best[:]), ALU.is_equal).then_inc(routed, 1)
                dve.wait_ge(routed, 6)
                dve.tensor_tensor(picked[:], one_hot[:], scores[:, :, 1:G], ALU.mult).then_inc(routed, 1)
                dve.wait_ge(routed, 7)
                dve.tensor_reduce(top_score[:], picked[:], AX.X, ALU.add).then_inc(routed, 1)
                dve.wait_ge(routed, 8)
                dve.tensor_tensor(top_score[:], scores[:, :, 0], top_score[:], ALU.subtract).then_inc(routed, 1)
                dve.wait_ge(exped, 1)
                dve.tensor_scalar(top_score[:], top_score[:], 1.0, None, ALU.add).then_inc(routed, 1)
                dve.wait_ge(routed, 10)
                dve.reciprocal(share[:], top_score[:]).then_inc(routed, 1)
                dve.wait_ge(routed, 11)
                dve.tensor_scalar(neg_share[:], share[:], -1.0, None, ALU.mult).then_inc(routed, 1)
                dve.tensor_tensor(coefs[:].rearrange("p e m -> p m e"), one_hot[:], over_experts(share[:]), ALU.mult)\
                   .then_inc(routed, 1)
                dve.wait_ge(routed, 13)

                def share_out(m):
                    dve.scalar_tensor_tensor(out=acc[:, m], in0=shared_sel[:, m], scalar=neg_share[:, m:m + 1],
                                             in1=acc[:, m], op0=ALU.mult, op1=ALU.add).then_inc(acc_done, 1)

                dve.wait_ge(shared_gathered, 16 * MT)
                dve.wait_ge(out_gathered, 16 * MT)
                for m in range(MT):
                    share_out(m)

                def step(i, s):
                    if not draining(i, s):
                        n = i * PAIR + (s + 1)
                        dve.wait_ge(silu_done, n)
                        dve.tensor_tensor(gated[:, s % RING], ps_u[:, s % 2, HF:D], gated[:, s % RING], ALU.mult)\
                           .then_inc(gated_done, 1)
                        dve.wait_ge(gated_done, n)
                        dve.bn_stats(z_stats[:, s % 2], gated[:, s % RING]).then_inc(stats_done, 1)
                        dve.wait_ge(stats_done, n)
                        dve.sem_inc(stats_seen, 1)
                        dve.bn_aggr(z_moments[:, s % 2], z_stats[:, s % 2]).then_inc(moments_done, 1)
                        dve.wait_ge(moments_done, n)
                        dve.tensor_scalar(z_var_eps[:, s % 2:s % 2 + 1], z_moments[:, s % 2, 1:2], EPS, None, ALU.add)\
                           .then_inc(eps_added, 1)
                    if s >= LAG_ACC:
                        k, slot = s - LAG_ACC, (s - LAG_ACC) // MT % 2
                        if k % MT == 0:
                            dve.wait_ge(acc_done, i * PAIR + (k + MT))
                            dve.tensor_copy(coef[:, slot:slot + 1], coefs[:, bass.ds(i * 2 + slot, 1)]).then_inc(coef_set, 1)
                            dve.wait_ge(coef_set, i * 2 + (slot + 1))
                        dve.wait_ge(down_done, i * PAIR + (k + 1))
                        dve.wait_ge(acc_done, i * PAIR + (k + 1))
                        t = k % MT
                        dve.scalar_tensor_tensor(out=acc[:, t], in0=ps_d[:, k % 2], scalar=coef[:, slot, t:t + 1],
                                                 in1=acc[:, t], op0=ALU.mult, op1=ALU.add).then_inc(acc_done, 1)
                    if not draining(i, s):
                        dve.wait_ge(rstd_done, i * PAIR + (s + 1))
                        dve.tensor_scalar(gated[:, s % RING], gated[:, s % RING], z_moments[:, s % 2, 0:1],
                                          z_rstd[:, s % 2:s % 2 + 1], ALU.subtract, ALU.mult).then_inc(normed, 1)
                    if s >= LAG_Z and not draining(i, s - LAG_Z):
                        k = s - LAG_Z
                        dve.wait_ge(zt_high, i * PAIR + (k + 1))
                        dve.tensor_tensor(zt_l[:, k % 2], ps_z[:, k % 2, 0:HF], zt_h[:, k % 2].bitcast(F32), ALU.subtract)\
                           .then_inc(zt_low, 1)
                    if s < PAIR:
                        e = i * 2 + (s // MT + 1)
                        slot = (s // MT + 1) % 2
                        if splits_next(i, s, 4):
                            split_w12(e, slot)
                        if splits_next(i, s, 5):
                            split_w3(e, slot)
                        if splits_next(i, s, 6):
                            split_bias(e, slot)

                steps(dve, step)

            @block.scalar
            def _(act):
                def split_w12(n, s, load):
                    act.wait_ge(loaded[s], load)
                    act.activation(w12_h[:, s], w12_raw[:, s], ACT.Copy).then_inc(w12_high, 1)

                def split_w3(n, s, load):
                    act.wait_ge(loaded[s], load)
                    act.activation(w3_h[:, s], w3_raw[:, s], ACT.Copy).then_inc(w3_high, 1)

                split_w12(0, 0, 16 * LOADS)
                split_w3(0, 0, 16 * LOADS)
                for m in range(MT):
                    act.wait_ge(ht_in_psum, m + 1)
                    act.activation(ht_h[:, :, m * P:(m + 1) * P], ps_t[:, m % 2], ACT.Copy).then_inc(ht_high, 1)
                act.wait_ge(biased_logits, MT)
                act.activation(scores[:], logits[:], ACT.Sigmoid).then_inc(scored, 1)
                act.wait_ge(routed, 9)
                act.activation(top_score[:], top_score[:], ACT.Exp).then_inc(exped, 1)

                def step(i, s):
                    if not draining(i, s):
                        act.wait_ge(up_done, i * PAIR + (s + 1))
                        if s >= RING:
                            act.wait_ge(zt_in_psum, i * PAIR + (s + 1 - RING))
                        act.activation(gated[:, s % RING], ps_u[:, s % 2, 0:HF], ACT.Silu).then_inc(silu_done, 1)
                    if s >= LAG_Z and not draining(i, s - LAG_Z):
                        k = s - LAG_Z
                        act.wait_ge(zt_in_psum, i * PAIR + (k + 1))
                        if k >= 2:
                            act.wait_ge(down_done, i * PAIR + (k - 1))
                        act.activation(zt_h[:, k % 2], ps_z[:, k % 2, 0:HF], ACT.Copy).then_inc(zt_high, 1)
                    if s < PAIR:
                        e = i * 2 + (s // MT + 1)
                        slot = (s // MT + 1) % 2
                        load = i * (16 * LOADS) + (2 - slot) * 16 * LOADS
                        if splits_next(i, s, 4):
                            act.wait_ge(down_done, i * PAIR + (s // MT * MT + 1))
                            split_w12(e, slot, load)
                        if splits_next(i, s, 5):
                            split_w3(e, slot, load)

                steps(act, step)

            @block.tensor
            def _(pe):
                PARTS = ((0, 0), (0, 1), (1, 0))
                ht, gate, zt = (ht_h, ht_l), (gate_h, gate_l), (zt_h, zt_l)
                w12, w3 = (w12_h, w12_l), (w3_h, w3_l)
                pe.wait_ge(small_loaded, 16 * SMALL)

                def logits_of(m):
                    pe.wait_ge(ht_low, m + 1)
                    pe.wait_ge(gate_split, 2)
                    if m >= 2:
                        pe.wait_ge(biased_logits, m - 1)
                    n = 0
                    for x, y in PARTS:
                        for c in range(DC):
                            mm = pe.matmul(ps_z[:, m % 2, 0:GP], ht[x][:, c, m * P:(m + 1) * P], gate[y][:, c],
                                           start=(n == 0), stop=(n == 3 * DC - 1))
                            n += 1
                    mm.then_inc(logits_in_psum, 1)

                pe.wait_ge(h_gathered, 16 * MT)
                for m in range(MT):
                    if m >= 2:
                        pe.wait_ge(ht_low, m - 1)
                    for c in range(DC):
                        mm = pe.transpose(ps_t[:, m % 2, c], h_sel[:, m, c * P:(c + 1) * P], ident[:])
                    mm.then_inc(ht_in_psum, 1)
                    if m:
                        logits_of(m - 1)
                logits_of(MT - 1)
                pe.wait_ge(biased_logits, MT)
                pe.wait_ge(consts, 6)

                def step(i, s):
                    if not draining(i, s):
                        slot, t = s // MT % 2, s % MT
                        if s % MT == 0:
                            pe.wait_ge(w12_low, i * 2 + (s // MT + 1))
                            pe.wait_ge(bias_low, i * 2 + (s // MT + 1))
                        if s >= 2:
                            pe.wait_ge(gated_done, i * PAIR + (s - 1))
                        pe.matmul(ps_u[:, s % 2], ones_rows[:], bias_rows[:, slot, 0:D], start=True, stop=False)
                        n = 0
                        for x, y in PARTS:
                            for c in range(DC):
                                mm = pe.matmul(ps_u[:, s % 2], ht[x][:, c, t * P:(t + 1) * P], w12[y][:, slot, c],
                                               start=False, stop=(n == 3 * DC - 1))
                                n += 1
                        mm.then_inc(up_done, 1)
                    if s >= LAG_Z and not draining(i, s - LAG_Z):
                        k = s - LAG_Z
                        pe.wait_ge(z_ready, i * PAIR + (k + 1))
                        if k >= 2:
                            pe.wait_ge(zt_low, i * PAIR + (k - 1))
                        for c in range(HC):
                            mm = pe.transpose(ps_z[:, k % 2, c * P:(c + 1) * P],
                                              gated[:, k % RING, c * P:(c + 1) * P], ident[:])
                        mm.then_inc(zt_in_psum, 1)
                    if s >= LAG_DOWN and not draining(i, s - LAG_DOWN):
                        k = s - LAG_DOWN
                        slot = k // MT % 2
                        if k % MT == 0:
                            pe.wait_ge(w3_low, i * 2 + (k // MT + 1))
                        pe.wait_ge(zt_low, i * PAIR + (k + 1))
                        if k >= 2:
                            pe.wait_ge(acc_done, i * PAIR + (MT + k - 1))
                        pe.matmul(ps_d[:, k % 2], ones_rows[:], bias_rows[:, slot, D:2 * D], start=True, stop=False)
                        n = 0
                        for x, y in PARTS:
                            for c in range(HC):
                                mm = pe.matmul(ps_d[:, k % 2], zt[x][:, k % 2, c * P:(c + 1) * P], w3[y][:, slot, c],
                                               start=False, stop=(n == 3 * HC - 1))
                                n += 1
                        mm.then_inc(down_done, 1)

                steps(pe, step)


def decoder_layer(nc, x_rows, wqk_t, wv_t, wo_t, ctx_t, xwq_t, xwk_t, xwv_t, xwo_t, xbq_cols, xbk_cols, xbv, xbo,
                  pad_rows, pad_cols, causal_q, causal_k, shared_w12_t, shared_b12, shared_w3_t, shared_b3,
                  shared_gamma, shared_beta, index_b, index_t, gate_t, gate_bias, exp_bias,
                  expert_w12_t, expert_w3_t, expert_bias, expert_gamma, expert_beta, eye, eye_bits, out_rows):
    scratch = lambda name, shape, dt=F32: nc.dram_tensor(name, shape, dt).ap()
    q_hi, q_lo, k_hi, k_lo = (scratch(n, (B, D, S)) for n in ("q_hi", "q_lo", "k_hi", "k_lo"))
    v_rows = scratch("v_rows", (B * S, H // 2, 3 * HD))
    attn_t, sums, inv_sums = scratch("attn_t", (B, D, S)), scratch("sums", (B * H, S)), scratch("inv_sums", (B * H, S))
    x1_rows = scratch("x1_rows", (B * S, D))
    q_parts = scratch("q_parts", (NBLK, H // 2, 3 * HD, 2, BLK))
    xk_parts = scratch("xk_parts", (3 * HD, B, H, SC))
    xv_ones = scratch("xv_ones", (B, KH, 2 * (H // 2) * 3 * HD))
    mask_q = scratch("mask_q", (P, B * 2 * TPB * SC), BF16)
    mask_k = scratch("mask_k", (KH, B * 2 * 2 * BLK), BF16)
    attn2_t, sums2, inv_sums2 = (scratch("attn2_t", (B, D, S)), scratch("sums2", (B * H, S)),
                                 scratch("inv_sums2", (B * H, S)))
    h_rows, shared_rows = scratch("h_rows", (B * S, D)), scratch("shared_rows", (B * S, D))
    eye_bf = eye_bits.bitcast(BF16)

    project_qkv(nc, x_rows, wqk_t, wv_t, eye, q_hi, q_lo, k_hi, k_lo, v_rows)
    self_attention(nc, q_hi, q_lo, k_hi, k_lo, v_rows, eye_bf, attn_t, sums)
    attention_to_queries(nc, x_rows, attn_t, sums, inv_sums, wo_t, xwq_t, xbq_cols, eye, x1_rows, q_parts)
    cross_context(nc, ctx_t, xwk_t, xwv_t, xbk_cols, xbv, pad_rows, pad_cols, causal_q, causal_k,
                  xk_parts, xv_ones, mask_q, mask_k)
    cross_attention(nc, q_parts, xk_parts, xv_ones, mask_q, mask_k, eye_bf, attn2_t, sums2)
    shared_feed_forward(nc, x1_rows, attn2_t, sums2, inv_sums2, xwo_t, xbo, shared_w12_t, shared_b12, shared_w3_t,
                        shared_b3, shared_gamma, shared_beta, eye, h_rows, shared_rows, out_rows)
    selected_experts(nc, h_rows, shared_rows, out_rows, index_b, index_t, gate_t, gate_bias, exp_bias,
                     expert_w12_t, expert_w3_t, expert_bias, expert_gamma, expert_beta, eye)


def kernel(**inputs):
    import numpy as np
    import concourse.bacc as bacc
    from concourse.bass_utils import run_bass_kernel_spmd

    a = {name: np.asarray(value) for name, value in inputs.items()}
    columns = lambda v: v.reshape(DC, P).T
    w_qkv = a["L0_attn_w_qkv"]
    pad = a["mask_BxS2_bf0"]
    hidden = np.where(np.arange(SC)[None] > np.arange(BLK)[:, None], np.float32(MASKED), np.float32(0))
    arrays = dict(
        x_rows=a["x"].reshape(B * S, D),
        wqk_t=w_qkv[:2 * D].T, wv_t=w_qkv[2 * D:].T, wo_t=a["L0_attn_w_out"].T,
        ctx_t=a["ctx_1024"].reshape(B * SC, D).T,
        xwq_t=a["L0_xattn_Wq"].T, xwk_t=a["L0_xattn_Wk"].T, xwv_t=a["L0_xattn_Wv"].T, xwo_t=a["L0_xattn_Wo"].T,
        xbq_cols=columns(a["L0_xattn_bq"]), xbk_cols=columns(a["L0_xattn_bk"]),
        xbv=a["L0_xattn_bv"], xbo=a["L0_xattn_bo"],
        pad_rows=pad, pad_cols=pad.reshape(B, 2, KH).transpose(2, 0, 1),
        causal_q=hidden.reshape(TPB, P, SC).transpose(1, 0, 2),
        causal_k=hidden.T.reshape(2, KH, BLK).transpose(1, 0, 2),
        shared_w12_t=np.concatenate([a["L0_ffn_sw1"], a["L0_ffn_sw2"]]).T,
        shared_b12=np.concatenate([a["L0_ffn_sb1"], a["L0_ffn_sb2"]]),
        shared_w3_t=a["L0_ffn_sw3"].T, shared_b3=a["L0_ffn_sb3"],
        shared_gamma=a["L0_ffn_s_ln_g"], shared_beta=a["L0_ffn_s_ln_b"],
        index_b=a["L0_ffn_index_b"].reshape(M // P, P).T, index_t=a["L0_ffn_index_t"].reshape(M // P, P).T,
        gate_t=np.concatenate([a["L0_ffn_sg_w"], a["L0_ffn_eg_w"]]).T,
        gate_bias=np.concatenate([a["L0_ffn_sg_b"], a["L0_ffn_eg_b"]]), exp_bias=a["L0_ffn_exp_bias"],
        expert_w12_t=np.concatenate([a["L0_ffn_ew1"], a["L0_ffn_ew2"]], axis=1).transpose(0, 2, 1),
        expert_w3_t=a["L0_ffn_ew3"].transpose(0, 2, 1),
        expert_bias=np.concatenate([a["L0_ffn_eb1"], a["L0_ffn_eb2"], a["L0_ffn_eb3"]], axis=1),
        expert_gamma=a["L0_ffn_sel_ln_g"], expert_beta=a["L0_ffn_sel_ln_b"],
        eye=np.eye(P, dtype=np.float32),
        eye_bits=np.eye(P, dtype=np.uint16) * np.uint16(0x3F80),
    )
    arrays = {name: np.ascontiguousarray(value) for name, value in arrays.items()}
    nc = bacc.Bacc("TRN2", target_bir_lowering=False, num_devices=1)
    args = [nc.dram_tensor("in_" + name, value.shape, mybir.dt.from_np(value.dtype), kind="ExternalInput").ap()
            for name, value in arrays.items()]
    out = nc.dram_tensor("out_rows", (B * S, D), F32, kind="ExternalOutput").ap()
    decoder_layer(nc, *args, out)
    result = run_bass_kernel_spmd(nc, [{"in_" + name: value for name, value in arrays.items()}], core_ids=[0])
    return result.results[0]["out_rows"].reshape(B, S, D)
```
